# Optimizing a Trainium2 kernel written in Bass

```python
import numpy as np
import jax
import jax.numpy as jnp

def _softmax(x, axis=-1):
    return jax.nn.softmax(x, axis=axis)

def _gelu(x):
    return jax.nn.gelu(x, approximate=True)

def _silu(x):
    return jax.nn.silu(x)

def _sigmoid(x):
    return jax.nn.sigmoid(x)

def _layernorm(x, axis=-1, eps=1e-05):
    m = jnp.mean(x, axis=axis, keepdims=True)
    v = jnp.var(x, axis=axis, keepdims=True)
    return (x - m) / jnp.sqrt(v + eps)

def _scatter_add(tgt, idx, src, axis=0):
    return tgt.at[idx].add(src)

def _segment_sum(src, seg, n):
    return jax.ops.segment_sum(src, seg, n)
kernel_name = 'mk_seq_preln_d1_jaxref_r4_0b0ce3'

def setup_inputs(seed: int=0):
    np.random.seed(seed)
    _w = jnp.asarray

    def _L0_attn_setup():
        import jax, jax.numpy as jnp
        import numpy as np
        B, T, D, H, S = (2, 512, 256, 16, 16)
        HD = D // H
        key = jax.random.key(seed)
        ks = jax.random.split(key, 8)
        x = jax.random.normal(ks[0], (B, T, D), dtype=jnp.float32)
        splat_centers = jax.random.normal(ks[1], (H, S, HD), dtype=jnp.float32) * 0.2
        splat_deltas = jnp.zeros((H, S, HD), dtype=jnp.float32)
        splat_log_scales = jax.random.normal(ks[2], (H, S), dtype=jnp.float32) * 0.2 + np.log(0.5).astype(np.float32)
        splat_log_amplitudes = jax.random.normal(ks[3], (H, S), dtype=jnp.float32) * 0.1 - 0.5
        movement_scale = jnp.asarray(0.08, dtype=jnp.float32)
        temperature = jnp.asarray(1.0, dtype=jnp.float32)
        lim_qkv = 0.5 * np.sqrt(6.0 / (D + 3 * D))
        qkv_w = jax.random.uniform(ks[4], (3 * D, D), dtype=jnp.float32, minval=-lim_qkv, maxval=lim_qkv)
        lim_out = 0.5 * np.sqrt(6.0 / (D + D))
        out_w = jax.random.uniform(ks[5], (D, D), dtype=jnp.float32, minval=-lim_out, maxval=lim_out)
        return {'x': x, 'splat_centers': splat_centers, 'splat_deltas': splat_deltas, 'splat_log_scales': splat_log_scales, 'splat_log_amplitudes': splat_log_amplitudes, 'movement_scale': movement_scale, 'temperature': temperature, 'qkv_w': qkv_w, 'out_w': out_w}
    _L0_attn_in = _L0_attn_setup()

    def _L0_ffn_setup():
        import jax, jax.numpy as jnp
        import numpy as np
        DIM = 256

        def _reference_tuple_inner(x, W_r, W_k, W_v, mu_r, mu_k):
            B, T, C = x.shape
            x_prev = jnp.concatenate([jnp.zeros((B, 1, C), x.dtype), x[:, :-1, :]], axis=1)
            xr = mu_r * x + (1.0 - mu_r) * x_prev
            xk = mu_k * x + (1.0 - mu_k) * x_prev
            r = jax.nn.sigmoid(jnp.einsum('btc,dc->btd', xr, W_r))
            k = jnp.einsum('btc,dc->btd', xk, W_k)
            k_act = jnp.square(jax.nn.relu(k))
            out = r * jnp.einsum('btc,dc->btd', k_act, W_v)
            new_state = x[:, -1, :]
            return (out, new_state)
        key = jax.random.key(seed)
        ks = jax.random.split(key, 6)
        B, T, C = (8, 512, DIM)
        x = jax.random.normal(ks[0], (B, T, C), dtype=jnp.float32)
        s = 1.0 / np.sqrt(C)
        W_r = jax.random.uniform(ks[1], (C, C), jnp.float32, -s, s)
        W_k = jax.random.uniform(ks[2], (C, C), jnp.float32, -s, s)
        W_v = jax.random.uniform(ks[3], (C, C), jnp.float32, -s, s)
        mu_r = jax.random.uniform(ks[4], (C,), jnp.float32)
        mu_k = jax.random.uniform(ks[5], (C,), jnp.float32)
        return {'x': x, 'W_r': W_r, 'W_k': W_k, 'W_v': W_v, 'mu_r': mu_r, 'mu_k': mu_k}
    _L0_ffn_in = _L0_ffn_setup()
    _d = {'L0_attn_x': _L0_attn_in['x'], 'L0_attn_splat_centers': _L0_attn_in['splat_centers'], 'L0_attn_splat_deltas': _L0_attn_in['splat_deltas'], 'L0_attn_splat_log_scales': _L0_attn_in['splat_log_scales'], 'L0_attn_splat_log_amplitudes': _L0_attn_in['splat_log_amplitudes'], 'L0_attn_movement_scale': _L0_attn_in['movement_scale'], 'L0_attn_temperature': _L0_attn_in['temperature'], 'L0_attn_qkv_w': _L0_attn_in['qkv_w'], 'L0_attn_out_w': _L0_attn_in['out_w'], 'L0_ffn_W_r': _L0_ffn_in['W_r'], 'L0_ffn_W_k': _L0_ffn_in['W_k'], 'L0_ffn_W_v': _L0_ffn_in['W_v'], 'L0_ffn_mu_r': _L0_ffn_in['mu_r'], 'L0_ffn_mu_k': _L0_ffn_in['mu_k']}
    _x0 = _d['L0_attn_x']
    _d['L0_attn_x'] = jax.random.normal(jax.random.fold_in(jax.random.key(seed), 1), (4, 2048, 256), dtype=_x0.dtype)
    del _x0
    return _d

def reference(L0_attn_x, L0_attn_splat_centers, L0_attn_splat_deltas, L0_attn_splat_log_scales, L0_attn_splat_log_amplitudes, L0_attn_movement_scale, L0_attn_temperature, L0_attn_qkv_w, L0_attn_out_w, L0_ffn_W_r, L0_ffn_W_k, L0_ffn_W_v, L0_ffn_mu_r, L0_ffn_mu_k):

    def _L0_attn_ref(x, splat_centers, splat_deltas, splat_log_scales, splat_log_amplitudes, movement_scale, temperature, qkv_w, out_w):
        import jax, jax.numpy as jnp
        import numpy as np
        B, T, D, H, S = (2, 512, 256, 16, 16)
        HD = D // H
        Bx, Tx, Dx = x.shape
        Hx, Sx, hd = splat_centers.shape
        qkv = (x @ qkv_w.T).reshape(Bx, Tx, 3, Hx, hd)
        q, k, v = (qkv[:, :, 0], qkv[:, :, 1], qkv[:, :, 2])
        centers = splat_centers + splat_deltas * jax.nn.sigmoid(movement_scale) * 0.2
        scales = jnp.clip(jnp.exp(splat_log_scales), 0.01, 2.0)
        amplitudes = jnp.clip(jnp.exp(splat_log_amplitudes), 1e-06, 10.0)
        inv_var = -0.5 / (scales ** 2 + 1e-08)
        q_dists = jnp.sum((q[:, :, :, None, :] - centers[None, None]) ** 2, axis=-1)
        k_dists = jnp.sum((k[:, :, :, None, :] - centers[None, None]) ** 2, axis=-1)
        q_weights = jnp.exp(q_dists * inv_var)
        k_weights = jnp.exp(k_dists * inv_var)
        logits = jnp.einsum('bihs,bjhs,hs->bijh', q_weights, k_weights, amplitudes)
        temp = jnp.clip(temperature, 0.1, 10.0)
        attention = jax.nn.softmax(logits / temp, axis=2)
        out = jnp.einsum('bijh,bjhd->bihd', attention, v).reshape(Bx, Tx, Dx)
        return out @ out_w.T

    def _L0_ffn_ref(x, W_r, W_k, W_v, mu_r, mu_k):
        import jax, jax.numpy as jnp
        import numpy as np
        DIM = 256

        def _reference_tuple_inner(x, W_r, W_k, W_v, mu_r, mu_k):
            B, T, C = x.shape
            x_prev = jnp.concatenate([jnp.zeros((B, 1, C), x.dtype), x[:, :-1, :]], axis=1)
            xr = mu_r * x + (1.0 - mu_r) * x_prev
            xk = mu_k * x + (1.0 - mu_k) * x_prev
            r = jax.nn.sigmoid(jnp.einsum('btc,dc->btd', xr, W_r))
            k = jnp.einsum('btc,dc->btd', xk, W_k)
            k_act = jnp.square(jax.nn.relu(k))
            out = r * jnp.einsum('btc,dc->btd', k_act, W_v)
            new_state = x[:, -1, :]
            return (out, new_state)
        return _reference_tuple_inner(x, W_r, W_k, W_v, mu_r, mu_k)[0]
    x = L0_attn_x
    x = x + _L0_attn_ref(_layernorm(x, axis=-1), L0_attn_splat_centers, L0_attn_splat_deltas, L0_attn_splat_log_scales, L0_attn_splat_log_amplitudes, L0_attn_movement_scale, L0_attn_temperature, L0_attn_qkv_w, L0_attn_out_w)
    x = x + _L0_ffn_ref(_layernorm(x, axis=-1), L0_ffn_W_r, L0_ffn_W_k, L0_ffn_W_v, L0_ffn_mu_r, L0_ffn_mu_k)
    return x

_drawn_inputs = setup_inputs


def setup_inputs(seed=0):
    import zlib

    import numpy as np

    out = dict(_drawn_inputs(seed))
    spreads = {'L0_attn_splat_deltas': (0.0, 0.8)}
    factors = {'L0_attn_splat_centers': 8.0,
     'L0_attn_splat_log_scales': 8.0,
     'L0_attn_splat_log_amplitudes': 8.0,
     'L0_attn_qkv_w': 8.0,
     'L0_attn_out_w': 8.0,
     'L0_ffn_W_r': 3.17,
     'L0_ffn_mu_r': 6.379}
    for name, (base, spread) in spreads.items():
        noise = np.random.default_rng([zlib.crc32(name.encode()), seed]).standard_normal(out[name].shape)
        drawn = base * np.exp(spread * noise) if base else spread * noise
        out[name] = jnp.asarray(drawn.astype(out[name].dtype))
    for name, factor in factors.items():
        out[name] = (out[name] * factor).astype(out[name].dtype)
    return out
```

```python
from contextlib import ExitStack

import concourse.bass as bass
from concourse import mybir

ALU = mybir.AluOpType
ACT = mybir.ActivationFunctionType
AX = mybir.AxisListType
F32 = mybir.dt.float32
BF16 = mybir.dt.bfloat16
I32 = mybir.dt.int32

P = 128
HEADS_AT_ONCE = 4
CHUNK = 512
BANKS_PER_GROUP = 3
SAFE_BOUND = 60.0
LN_EPS = 1e-5
RSQRT_SEED = 0x5F3759DF
NEWTON = 3
LN_STEPS = 4 + 4 + 3 + 4 * NEWTON + 4
Q_TERMS = [0, 0, 1, 1, 0, 2]
K_TERMS = [0, 1, 0, 1, 2, 0]
TERMS = len(Q_TERMS)


class Count:

    def __init__(self, before):
        self.before, self.steps = before, 0

    def step(self):
        self.steps += 1
        return 1

    def total(self):
        return self.before + self.steps


def groups_of(units):
    found, at = [], 0
    while units - at > 4 or units - at == 3:
        found.append((at, BANKS_PER_GROUP))
        at += BANKS_PER_GROUP
    while at < units:
        found.append((at, 2))
        at += 2
    return found


def preln_block(nc, x, qkv_wT, out_wT, r_wT, k_wT, v_wT, cen_hds, del_hds, cen_hsd, del_hsd,
                log_scales, log_amps, movement, temperature, mu_r, mu_k, ident_in, headmask_in,
                rowmask_in, out):
    NB, T, D = x.shape
    S = cen_hds.shape[1]
    NC = T // CHUNK
    KT = T // P
    TT = CHUNK // P
    HALVES = D // P
    STAGES = 2 * HALVES
    UNITS = NC * STAGES
    TILES = KT * HEADS_AT_ONCE
    GROUPS = groups_of(TILES)
    NG = len(GROUPS)
    SHIFT_ROW = TERMS * S
    ROWS = SHIFT_ROW + 1
    LOADS = 16 * (2 * TERMS + NC)
    assert NG % 2 == 0 and S == 16 and NC == STAGES == 4

    PREP_STEPS = {1: 6, 2: 4, 3: 2}
    PREP_BEFORE = {1: 0, 2: 6 * NC, 3: 10 * NC}
    PREP_TOTAL = 12 * NC
    FFN_STEPS = 10
    MAX_TILES = KT * HEADS_AT_ONCE * NC + 1
    MAX_STEPS = KT * HEADS_AT_ONCE * (NC + 1) + 1
    PREP_AT = {1: [8, 9, 11, 12, 14, 16], 2: [7, 9, 11, 13], 3: [8, 10]}
    FFN_AT = [5, 6, 12, 13, 15, 16, 17, 18, 20, 21]

    x_rows = x.rearrange("b t d -> (b t) d")
    out_rows = out.rearrange("b t d -> (b t) d")

    with ExitStack() as ctx:
        def sb(name, shape, dt=F32):
            return ctx.enter_context(nc.sbuf_tensor(name, shape, dt))

        def sem(name):
            return ctx.enter_context(nc.semaphore(name))

        wqkv = sb("wqkv", [P, HALVES, 3 * D])
        wout = sb("wout", [P, HALVES, D])
        wr = sb("wr", [P, HALVES, D])
        wk = sb("wk", [P, HALVES, D])
        wv = sb("wv", [P, HALVES, D])
        ident = sb("ident", [P, P])
        headmask = sb("headmask", [P, P])
        rowmask = sb("rowmask", [P, 2])
        cen_t = sb("cen_t", [P, HALVES, S])
        del_t = sb("del_t", [P, HALVES, S])
        cen_n = sb("cen_n", [P, HALVES, S])
        del_n = sb("del_n", [P, HALVES, S])
        cross = sb("cross", [P, HALVES, P])
        cen_sq = sb("cen_sq", [P, HALVES])
        inv_var = sb("inv_var", [P, HALVES])
        amp = sb("amp", [P, HALVES])
        bound = sb("bound", [P, HALVES])
        params = sb("params", [P, 2])
        mu = sb("mu", [P, 2, HALVES])
        one_minus_mu = sb("one_minus_mu", [P, 2, HALVES])
        flag_f = sb("flag_f", [1, 2])
        flag = sb("flag", [1, 1], I32)
        shift = sb("shift", [P, HALVES, CHUNK], BF16)
        k_aug = sb("k_aug", [ROWS, 2, HEADS_AT_ONCE, T], BF16)
        q_aug = sb("q_aug", [ROWS, 2, HEADS_AT_ONCE, T], BF16)
        vals = sb("vals", [P, 2, KT, HEADS_AT_ONCE, 32])
        probs = sb("probs", [P, 2, BANKS_PER_GROUP, CHUNK])
        o_raw = sb("o_raw", [P, CHUNK])
        den = sb("den", [P, CHUNK])
        attn = sb("attn", [P, HALVES, T])
        staged = sb("staged", [P, HALVES, CHUNK])
        xin = sb("xin", [P, TT, D])
        h = sb("h", [P, TT, D])
        stats = sb("stats", [P, TT, 6])
        moments = sb("moments", [P, TT, 2])
        ln_v = sb("ln_v", [P, TT])
        ln_y = sb("ln_y", [P, TT])
        ln_a = sb("ln_a", [P, TT])
        h_t = sb("h_t", [P, HALVES, T])
        v_all = sb("v_all", [P, KT, D])
        qk = sb("qk", [P, HALVES, CHUNK])
        qk_sq = sb("qk_sq", [P, HALVES, CHUNK])
        weight = sb("weight", [P, HALVES, CHUNK])
        tmp = sb("tmp", [P, CHUNK])
        rest = tmp
        parts = sb("parts", [P, 3, CHUNK], BF16)
        h2_t = sb("h2_t", [P, HALVES, 1 + CHUNK])
        mixed_r, mixed_k = qk, qk_sq
        k_act = sb("k_act", [P, HALVES, CHUNK])
        gate_in = sb("gate_in", [P, TT, D])
        gate = weight[:, :, :].rearrange("p a (n d) -> p (a n) d", d=D)
        tile_max = sb("tile_max", [P, NC])
        row_max = sb("row_max", [P, HEADS_AT_ONCE * KT])
        max_rows = sb("max_rows", [HEADS_AT_ONCE * KT, P], BF16)

        ps_scores = ctx.enter_context(nc.psum_tensor("ps_scores", [P, 2, BANKS_PER_GROUP, CHUNK], F32))
        ps_pv = ctx.enter_context(nc.psum_tensor("ps_pv", [P, CHUNK], F32))
        ps_step = ctx.enter_context(nc.psum_tensor("ps_step", [P, CHUNK], F32))

        q_parts = nc.dram_tensor("q_parts", [NB, 3, D, T], BF16, kind="Internal").ap()
        k_parts = nc.dram_tensor("k_parts", [NB, 3, D, T], BF16, kind="Internal").ap()

        consts_loaded = sem("consts_loaded")
        ones_set = sem("ones_set")
        setup_dve = sem("setup_dve")
        setup_act = sem("setup_act")
        setup_pe = sem("setup_pe")
        aug_loaded = sem("aug_loaded")
        scores_ready = sem("scores_ready")
        probs_ready = sem("probs_ready")
        pv_done = sem("pv_done")
        pv_free = sem("pv_free")
        vals_staged = sem("vals_staged")
        norm_steps = sem("norm_steps")
        chunk_normed = sem("chunk_normed")
        prep_x_loaded = sem("prep_x_loaded")
        prep_ln = sem("prep_ln")
        prep_mm = sem("prep_mm")
        prep_free = sem("prep_free")
        squared = sem("squared")
        weighted = sem("weighted")
        q_split = sem("q_split")
        k_split = sem("k_split")
        parts_stored = sem("parts_stored")
        h_staged = sem("h_staged")
        ffn_x_loaded = sem("ffn_x_loaded")
        attn_staged = sem("attn_staged")
        ffn_ln = sem("ffn_ln")
        ffn_mm = sem("ffn_mm")
        ffn_free = sem("ffn_free")
        carry_cleared = sem("carry_cleared")
        mix_steps = sem("mix_steps")
        act_steps = sem("act_steps")
        gate_exp = sem("gate_exp")
        gate_steps = sem("gate_steps")
        out_stored = sem("out_stored")
        max_mm = sem("max_mm")
        max_free = sem("max_free")
        max_stored = sem("max_stored")

        counts = {id(eng): eng.alloc_register("waited_count") for eng in (nc.sync, nc.tensor, nc.vector, nc.gpsimd)}

        def wait_alone(eng, on, count):
            if not isinstance(count, int):
                eng.reg_mov(counts[id(eng)], count)
                count = counts[id(eng)]
            eng.wait_ge(consts_loaded, 16 * N_CONSTS)
            eng.wait_ge(on, count)

        def prep_count(batch, stage, i, k=0):
            return PREP_TOTAL * batch + PREP_BEFORE[stage] + PREP_STEPS[stage] * i + k

        def weight_count(batch, stage, i, half=0):
            return 4 * NC * batch + 2 * NC * (stage - 1) + 2 * i + half

        def ffn_count(batch, i, k=0):
            return FFN_STEPS * (NC * batch + i) + k

        NORM = (2, 4)

        def norm_count(b, s, i):
            return NC * (b * HALVES * sum(NORM) + s // 2 * sum(NORM) + s % 2 * NORM[0]) + NORM[s % 2] * i

        def batches(eng, body):
            body(0, True, False)
            with eng.Fori(1, NB - 1) as b:
                body(b, True, True)
            body(NB - 1, False, True)

        block = ctx.enter_context(nc.Block())

        @block.sync
        def _(sp):
            consts = [
                (ident[:, :], ident_in), (headmask[:, :], headmask_in), (rowmask[:, :], rowmask_in),
                (params[:, 0:1], movement.broadcast_to([P, 1])),
                (params[:, 1:2], temperature.broadcast_to([P, 1])),
                (inv_var[:, :], log_scales),
                (amp[:, :], log_amps),
                (cen_t[:, :, :], cen_hds.rearrange("(a p) s -> p a s", p=P)),
                (del_t[:, :, :], del_hds.rearrange("(a p) s -> p a s", p=P)),
                (cen_n[:, :, :], cen_hsd.rearrange("(a p) s -> p a s", p=P)),
                (del_n[:, :, :], del_hsd.rearrange("(a p) s -> p a s", p=P)),
                (mu[:, 0, :], mu_r),
                (mu[:, 1, :], mu_k),
                (wqkv[:, :, :], qkv_wT.rearrange("(a p) n -> p a n", p=P)),
                (wout[:, :, :], out_wT.rearrange("(a p) n -> p a n", p=P)),
                (wr[:, :, :], r_wT.rearrange("(a p) n -> p a n", p=P)),
                (wk[:, :, :], k_wT.rearrange("(a p) n -> p a n", p=P)),
                (wv[:, :, :], v_wT.rearrange("(a p) n -> p a n", p=P)),
            ]
            assert len(consts) == N_CONSTS

            def load_x(batch, i, landed):
                rows = x_rows[bass.ds(batch * T + i * CHUNK, CHUNK), :]
                sp.dma_start(out=xin[:, :, :], in_=rows.rearrange("(n p) d -> p n d", p=P)).then_inc(landed, 16)

            def store_parts(batch, stage, i):
                dram, split, steps = (q_parts, q_split, 4) if stage == 1 else (k_parts, k_split, 5)
                for half in range(HALVES):
                    nth = 2 * NC * batch + 2 * i + half
                    wait_alone(sp, split, steps * (nth + 1))
                    to = dram[bass.ds(batch, 1), :, half * P:(half + 1) * P, bass.ds(i * CHUNK, CHUNK)]
                    sp.dma_start(out=to.rearrange("o k p t -> p (o k) t"), in_=parts[:, :, :]).then_inc(parts_stored, 16)

            def load_aug(batch, stage, after):
                half, odd = stage // 2, stage % 2
                for dram, aug, terms in ((q_parts, q_aug, Q_TERMS), (k_parts, k_aug, K_TERMS)):
                    for j, part in enumerate(terms):
                        rows = dram[bass.ds(batch, 1), part, half * P:(half + 1) * P, :]
                        rows = rows.rearrange("o (c e s) t -> (o s) c e t", e=2, s=S)[:, :, odd, :]
                        sp.dma_start(out=aug[j * S:(j + 1) * S, odd, :, :], in_=rows).then_inc(aug_loaded, 16)
                first = odd * S
                for i in range(NC):
                    sp.dma_start(out=q_aug[SHIFT_ROW:ROWS, odd, :, i * CHUNK:(i + 1) * CHUNK],
                                 in_=shift[first:P:2 * S, half, :]).then_inc(aug_loaded, 16)

            def prep_dmas(batch, stage, i):
                if stage == 1:
                    sp.wait_ge(prep_ln, LN_STEPS * (NC * batch + i))
                    load_x(batch, i, prep_x_loaded)
                if stage in (1, 2):
                    store_parts(batch, stage, i)

            def ffn_dmas(batch, i):
                sp.wait_ge(gate_steps, 3 * (NC * batch + i))
                load_x(batch, i, ffn_x_loaded)
                sp.wait_ge(gate_steps, 3 * (NC * batch + i + 1))
                rows = out_rows[bass.ds(batch * T + i * CHUNK, CHUNK), :]
                sp.dma_start(out=rows.rearrange("(n p) d -> p n d", p=P), in_=gate_in[:, :, :]).then_inc(out_stored, 16)

            for to, of in consts:
                sp.dma_start(out=to, in_=of).then_inc(consts_loaded, 16)
            for stage in (1, 2):
                with sp.Fori(0, NC) as i:
                    prep_dmas(0, stage, i)
            sp.wait_ge(setup_dve, SETUP_SHIFT)
            sp.wait_ge(parts_stored, 16 * 4 * NC)
            load_aug(0, 0, 0)

            def body(b, prep, ffn):
                for s in range(STAGES):
                    if s < STAGES - 1 or prep:
                        nb, ns = (b, s + 1) if s < STAGES - 1 else (b + 1, 0)
                        wait_alone(sp, aug_loaded, LOADS * (STAGES * b + s + 1))
                        if s > 0:
                            sp.wait_ge(probs_ready, NG * NC * (STAGES * b + s))
                        elif ffn:
                            sp.wait_ge(probs_ready, NG * NC * (STAGES * b))
                        if s == STAGES - 1:
                            wait_alone(sp, parts_stored, 16 * 4 * NC * (nb + 1))
                        load_aug(nb, ns, STAGES * b + s)
                    if (s == 0 and ffn) or (s in (1, 2) and prep):
                        with sp.Fori(0, NC) as i:
                            if s == 0:
                                ffn_dmas(b - 1, i)
                            else:
                                if s == 1 and ffn:
                                    sp.wait_ge(gate_steps, 3 * NC * b)
                                prep_dmas(b + 1, s, i)

            batches(sp, body)
            with sp.Fori(0, NC) as i:
                ffn_dmas(NB - 1, i)
            sp.wait_ge(out_stored, 16 * NC * NB)

        @block.tensor
        def _(pe):
            def scores(g, par, query, last_inc=True):
                first, n = GROUPS[g]
                for m in range(n):
                    kt, c = divmod(first + m, HEADS_AT_ONCE)
                    mm = pe.matmul(ps_scores[:, g % 2, m, :], k_aug[:, par, c, kt * P:(kt + 1) * P],
                                   q_aug[:, par, c, bass.ds(query, CHUNK)], start=True, stop=True)
                mm.then_inc(scores_ready, 1)

            def values(g, par):
                first, n = GROUPS[g]
                for m in range(n):
                    kt, c = divmod(first + m, HEADS_AT_ONCE)
                    mm = pe.matmul(ps_pv[32 * c:32 * c + 32, :], vals[:, par, kt, c, :], probs[:, g % 2, m, :],
                                   start=(kt == 0), stop=(kt == KT - 1))
                if g == NG - 1:
                    mm.then_inc(pv_done, 1)

            def turn(src, half):
                for n in range(TT):
                    mm = pe.transpose(ps_step[:, n * P:(n + 1) * P], src[:, n, half * P:(half + 1) * P], ident[:, :])
                return mm

            def rows_out(lhs, w, pair, cols):
                for m in range(2):
                    n = 2 * pair + m
                    for half in range(HALVES):
                        mm = pe.matmul(ps_step[:, m * D:(m + 1) * D], lhs[:, half, n * P:(n + 1) * P],
                                       w[:, half, cols:cols + D], start=(half == 0), stop=(half == HALVES - 1))
                return mm

            def prep_step(batch, stage, i, k):
                pe.wait_ge(prep_free, prep_count(batch, stage, i, k))
                if stage == 1 and k < 2:
                    if k == 0:
                        pe.wait_ge(prep_ln, LN_STEPS * (NC * batch + i + 1))
                    mm = turn(h, k)
                elif stage == 3:
                    if k == 0:
                        pe.wait_ge(h_staged, NC * batch + i + 1)
                    mm = rows_out(staged, wqkv, k, 2 * D)
                else:
                    k -= 2 if stage == 1 else 0
                    if k < HALVES:
                        for half in range(HALVES):
                            mm = pe.matmul(ps_step[:, :], wqkv[:, half, (stage - 1) * D + k * P:(stage - 1) * D + (k + 1) * P],
                                           h_t[:, half, bass.ds(i * CHUNK, CHUNK)], start=(half == 0), stop=(half == 1))
                    else:
                        k -= HALVES
                        pe.wait_ge(squared, weight_count(batch, stage, i, k) + 1)
                        pe.matmul(ps_step[:, :], headmask[:, :], qk_sq[:, k, :], start=True, stop=False)
                        mm = pe.matmul(ps_step[:, :], cross[:, k, :], qk[:, k, :], start=False, stop=True)
                mm.then_inc(prep_mm, 1)

            def ffn_step(batch, i, k):
                pe.wait_ge(ffn_free, ffn_count(batch, i, k))
                if k < 2:
                    if k == 0:
                        pe.wait_ge(attn_staged, NC * batch + i + 1)
                    mm = rows_out(staged, wout, k, 0)
                elif k < 4:
                    if k == 2:
                        pe.wait_ge(ffn_ln, LN_STEPS * (NC * batch + i + 1))
                    mm = turn(h, k - 2)
                elif k < 6:
                    if k == 4:
                        pe.wait_ge(mix_steps, 9 * (NC * batch + i) + 5)
                    for half in range(HALVES):
                        mm = pe.matmul(ps_step[:, :], wk[:, half, (k - 4) * P:(k - 3) * P], mixed_k[:, half, :],
                                       start=(half == 0), stop=(half == 1))
                elif k < 8:
                    if k == 6:
                        pe.wait_ge(mix_steps, 9 * (NC * batch + i + 1))
                    mm = rows_out(mixed_r, wr, k - 6, 0)
                else:
                    if k == 8:
                        pe.wait_ge(act_steps, 2 * (NC * batch + i + 1))
                    mm = rows_out(k_act, wv, k - 8, 0)
                mm.then_inc(ffn_mm, 1)

            def shift_pass(stage_no, par):
                with pe.Fori(0, KT) as qt:
                    for n in range(HEADS_AT_ONCE * NC):
                        c, kc = divmod(n, NC)
                        pe.wait_ge(max_free, MAX_STEPS * stage_no + HEADS_AT_ONCE * (NC + 1) * qt + (NC + 1) * c + kc)
                        pe.matmul(ps_step[:, :], q_aug[0:SHIFT_ROW, par, c, bass.ds(qt * P, P)],
                                  k_aug[0:SHIFT_ROW, par, c, kc * CHUNK:(kc + 1) * CHUNK], start=True, stop=True
                                  ).then_inc(max_mm, 1)
                wait_alone(pe, max_free, MAX_STEPS * (stage_no + 1) - 1)
                pe.transpose(ps_step[0:HEADS_AT_ONCE * KT, 0:P], row_max[:, :], ident[:, :]).then_inc(max_mm, 1)
                pe.wait_ge(max_free, MAX_STEPS * (stage_no + 1))
                pe.wait_ge(max_stored, 16 * (stage_no + 1))

            pe.wait_ge(consts_loaded, 16 * N_CONSTS)
            pe.wait_ge(setup_dve, SETUP_AMP)
            pe.matmul(ps_step[:, 0:HALVES], headmask[:, :], amp[:, :], start=True, stop=True).then_inc(setup_pe, 1)
            pe.wait_ge(setup_dve, SETUP_BOUND)
            for half in range(HALVES):
                mm = pe.matmul(ps_step[0:1, half * P:(half + 1) * P], bound[:, half:half + 1], ident[:, :],
                               start=True, stop=True)
            mm.then_inc(setup_pe, 1)
            pe.wait_ge(setup_dve, SETUP_STEPS)
            unsafe = pe.value_load(flag[0:1, 0:1], min_val=0, max_val=1)

            for stage in (1, 2, 3):
                with pe.Fori(0, NC) as i:
                    for k in range(PREP_STEPS[stage]):
                        prep_step(0, stage, i, k)

            pe.wait_ge(aug_loaded, LOADS)
            pe.wait_ge(ones_set, 2)
            pe.wait_ge(prep_free, PREP_TOTAL)
            with pe.If(unsafe == 1):
                shift_pass(0, 0)
            scores(0, 0, 0)
            scores(1, 0, 0)

            def unit(b, s, i, prep, ffn, ends=False):
                par = s % 2
                last_stage = s == STAGES - 1 and not prep
                if not last_stage:
                    with pe.If(unsafe * i == NC - 1):
                        pe.wait_ge(aug_loaded, LOADS * (STAGES * b + s + 2))
                        if s == 0 and ffn:
                            wait_alone(pe, ffn_free, ffn_count(b - 1, i))
                        elif s > 0 and prep:
                            wait_alone(pe, prep_free, prep_count(b + 1, s, i))
                        elif ffn:
                            wait_alone(pe, ffn_free, ffn_count(b, 0))
                        shift_pass(STAGES * b + s + 1, 1 - par)
                u = UNITS * b + NC * s + i
                turn_over = 0 if ends or last_stage else (i + 1) >> 2
                for g in range(NG):
                    pe.wait_ge(probs_ready, NG * u + g + 1)
                    if g == 0:
                        pe.wait_ge(pv_free, u)
                        pe.wait_ge(vals_staged, NC * (STAGES * b + s + 1))
                    values(g, par)
                    if g + 2 < NG:
                        scores(g + 2, par, i * CHUNK)
                    elif not ends:
                        if g + 2 == NG:
                            wait_alone(pe, aug_loaded, LOADS * (STAGES * b + s + 1 + turn_over))
                        flip = turn_over if par == 0 else 1 - turn_over
                        scores_next(g + 2 - NG, flip, ((i + 1) & 3) * CHUNK)
                    if ffn and s == 0 and g in FFN_AT:
                        ffn_step(b - 1, i, FFN_AT.index(g))
                    if prep and s > 0 and g in PREP_AT[s]:
                        if s == 1 and ffn and g == PREP_AT[s][0]:
                            pe.wait_ge(ffn_free, ffn_count(b, 0))
                        prep_step(b + 1, s, i, PREP_AT[s].index(g))

            def scores_next(g, par, query):
                first, n = GROUPS[g]
                for m in range(n):
                    kt, c = divmod(first + m, HEADS_AT_ONCE)
                    keys = k_aug[:, bass.ds(par, 1), c, kt * P:(kt + 1) * P].rearrange("r o t -> r (o t)")
                    queries = q_aug[:, bass.ds(par, 1), c, bass.ds(query, CHUNK)].rearrange("r o t -> r (o t)")
                    mm = pe.matmul(ps_scores[:, g % 2, m, :], keys, queries, start=True, stop=True)
                mm.then_inc(scores_ready, 1)

            def body(b, prep, ffn):
                for s in range(STAGES):
                    if s == 0 and ffn:
                        wait_alone(pe, prep_free, PREP_TOTAL * (b + 1))
                    if s == STAGES - 1 and not prep:
                        with pe.Fori(0, NC - 1) as i:
                            unit(b, s, i, prep, ffn)
                        unit(b, s, NC - 1, prep, ffn, ends=True)
                    else:
                        with pe.Fori(0, NC) as i:
                            unit(b, s, i, prep, ffn)

            batches(pe, body)
            with pe.Fori(0, NC) as i:
                for k in range(FFN_STEPS):
                    ffn_step(NB - 1, i, k)

        @block.scalar
        def _(act):
            def probabilities(b, s, i, g):
                n = GROUPS[g][1]
                act.wait_ge(scores_ready, NG * (UNITS * b + NC * s + i) + g + 1)
                act.activation(probs[:, g % 2, 0:n, :], ps_scores[:, g % 2, 0:n, :], ACT.Exp).then_inc(probs_ready, 1)

            def splat_exp(batch, stage, i, half):
                k = (4 if stage == 1 else 2) + half
                act.wait_ge(prep_free, prep_count(batch, stage, i, k) + 1)
                act.activation(weight[:, half, :], weight[:, half, :], ACT.Exp,
                               scale=inv_var[:, half:half + 1]).then_inc(weighted, 1)

            def gate_exponential(batch, i, pair):
                act.wait_ge(ffn_free, ffn_count(batch, i, 6 + pair) + 1)
                act.activation(gate[:, 2 * pair:2 * pair + 2, :], gate_in[:, 2 * pair:2 * pair + 2, :],
                               ACT.Exp, scale=-1.0).then_inc(gate_exp, 1)

            act.wait_ge(consts_loaded, 16 * N_CONSTS)
            act.activation(params[:, 0:1], params[:, 0:1], ACT.Exp, scale=-1.0).then_inc(setup_act, 1)
            act.activation(inv_var[:, :], inv_var[:, :], ACT.Exp).then_inc(setup_act, 1)
            act.activation(amp[:, :], amp[:, :], ACT.Exp).then_inc(setup_act, 1)
            act.wait_ge(setup_dve, SETUP_STEPS)
            for stage in (1, 2):
                with act.Fori(0, NC) as i:
                    for half in range(HALVES):
                        splat_exp(0, stage, i, half)

            def body(b, prep, ffn):
                for s in range(STAGES):
                    with act.Fori(0, NC) as i:
                        for g in range(NG):
                            probabilities(b, s, i, g)
                            if prep and s in (1, 2):
                                for half in range(HALVES):
                                    if g == PREP_AT[s][-2 + half] + 1:
                                        splat_exp(b + 1, s, i, half)
                            if ffn and s == 0:
                                for pair in range(2):
                                    if g == FFN_AT[6 + pair] + 1:
                                        gate_exponential(b - 1, i, pair)

            batches(act, body)
            with act.Fori(0, NC) as i:
                for pair in range(2):
                    gate_exponential(NB - 1, i, pair)

        @block.gpsimd
        def _(pool):
            def stage_values(batch, stage, i, count):
                half, odd = stage // 2, stage % 2
                src = v_all[:, bass.ds(i * TT, TT), half * P:(half + 1) * P]
                src = src.rearrange("p k (c e d) -> p k c e d", e=2, d=16)
                for c in range(HEADS_AT_ONCE):
                    cp = pool.tensor_copy(vals[:, odd, bass.ds(i * TT, TT), c, 16 * odd:16 * odd + 16],
                                          src[:, :, c, odd, :])
                cp.then_inc(vals_staged, 1)

            def stage_h(batch, i):
                pool.wait_ge(prep_free, prep_count(batch, 3, i))
                pool.tensor_copy(staged[:, :, :], h_t[:, :, bass.ds(i * CHUNK, CHUNK)]).then_inc(h_staged, 1)

            def stage_attn(batch, i):
                pool.wait_ge(ffn_mm, ffn_count(batch, i))
                pool.tensor_copy(staged[:, :, :], attn[:, :, bass.ds(i * CHUNK, CHUNK)]).then_inc(attn_staged, 1)

            def store_max(stage_no, par):
                wait_alone(pool, max_free, MAX_STEPS * (stage_no + 1))
                to = q_aug[SHIFT_ROW:ROWS, par, :, :].rearrange("o c (k t) -> o (c k) t", t=P)
                pool.dma_start(out=to, in_=max_rows[:, :]).then_inc(max_stored, 16)

            pool.memset(k_aug[SHIFT_ROW:ROWS, :, :, :], 1.0).then_inc(ones_set, 1)
            pool.wait_ge(setup_dve, SETUP_STEPS)
            unsafe = pool.value_load(flag[0:1, 0:1], min_val=0, max_val=1)
            pool.wait_ge(ones_set, 2)
            with pool.Fori(0, NC) as i:
                stage_h(0, i)
                pool.wait_ge(prep_free, prep_count(0, 3, i) + PREP_STEPS[3])
                stage_values(0, 0, i, 0)
            with pool.If(unsafe == 1):
                store_max(0, 0)

            def body(b, prep, ffn):
                for s in range(STAGES):
                    par = s % 2
                    if s == STAGES - 1 and not prep:
                        continue
                    with pool.Fori(0, NC) as i:
                        with pool.If(unsafe * i == NC - 1):
                            store_max(STAGES * b + s + 1, 1 - par)
                        if s == 0 and ffn:
                            pool.wait_ge(chunk_normed, UNITS * b + i)
                            stage_attn(b - 1, i)
                        if s == STAGES - 1:
                            stage_h(b + 1, i)
                            pool.wait_ge(prep_free, prep_count(b + 1, 3, i) + PREP_STEPS[3])
                        if s > 0:
                            pool.wait_ge(pv_done, UNITS * b + NC * s)
                        elif ffn:
                            pool.wait_ge(pv_done, UNITS * b)
                        if s == STAGES - 1:
                            stage_values(b + 1, 0, i, 0)
                        else:
                            stage_values(b, s + 1, i, 0)

            batches(pool, body)
            pool.wait_ge(chunk_normed, UNITS * NB)
            with pool.Fori(0, NC) as i:
                stage_attn(NB - 1, i)

        @block.vector
        def _(v):
            even_den = [16 + i % 16 for i in range(32)]
            odd_den = [i % 16 for i in range(32)]

            def layernorm(nth, steps_sem):
                n = Count(LN_STEPS * nth)
                v.wait_ge(steps_sem, n.total())
                for t in range(TT):
                    v.bn_stats(out=stats[:, t, :], in_=xin[:, t, :]).then_inc(steps_sem, n.step())
                wait_alone(v, steps_sem, n.total())
                for t in range(TT):
                    v.bn_aggr(out=moments[:, t, :], in_=stats[:, t, :]).then_inc(steps_sem, n.step())
                v.wait_ge(steps_sem, n.total())
                v.tensor_scalar(ln_v[:, :], moments[:, :, 1], LN_EPS, None, ALU.add).then_inc(steps_sem, n.step())
                v.wait_ge(steps_sem, n.total())
                v.tensor_scalar(ln_a[:, :].bitcast(I32), ln_v[:, :].bitcast(I32), 1, None,
                                ALU.logical_shift_right).then_inc(steps_sem, n.step())
                v.wait_ge(steps_sem, n.total())
                v.tensor_scalar(ln_y[:, :].bitcast(I32), ln_a[:, :].bitcast(I32), -1.0, float(RSQRT_SEED),
                                ALU.mult, ALU.add).then_inc(steps_sem, n.step())
                for _ in range(NEWTON):
                    v.wait_ge(steps_sem, n.total())
                    v.tensor_tensor(ln_a[:, :], ln_y[:, :], ln_v[:, :], ALU.mult).then_inc(steps_sem, n.step())
                    v.wait_ge(steps_sem, n.total())
                    v.tensor_tensor(ln_a[:, :], ln_a[:, :], ln_y[:, :], ALU.mult).then_inc(steps_sem, n.step())
                    v.wait_ge(steps_sem, n.total())
                    v.tensor_scalar(ln_a[:, :], ln_a[:, :], -0.5, 1.5, ALU.mult, ALU.add).then_inc(steps_sem, n.step())
                    v.wait_ge(steps_sem, n.total())
                    v.tensor_tensor(ln_y[:, :], ln_y[:, :], ln_a[:, :], ALU.mult).then_inc(steps_sem, n.step())
                v.wait_ge(steps_sem, n.total())
                for t in range(TT):
                    v.tensor_scalar(h[:, t, :], xin[:, t, :], moments[:, t, 0:1], ln_y[:, t:t + 1],
                                    ALU.subtract, ALU.mult).then_inc(steps_sem, n.step())
                assert n.steps == LN_STEPS

            def split(batch, stage, i, half):
                sem_, per = (q_split, 4) if stage == 1 else (k_split, 5)
                n = Count(per * (2 * NC * batch + 2 * i + half))
                v.wait_ge(sem_, n.total())
                v.wait_ge(weighted, weight_count(batch, stage, i, half) + 1)
                if stage == 2:
                    v.tensor_scalar(weight[:, half, :], weight[:, half, :], amp[:, half:half + 1], None,
                                    ALU.mult).then_inc(sem_, n.step())
                    v.wait_ge(sem_, n.total())
                v.wait_ge(parts_stored, 16 * weight_count(batch, stage, i, half))
                v.tensor_copy(parts[:, 0, :], weight[:, half, :]).then_inc(sem_, n.step())
                v.wait_ge(sem_, n.total())
                v.tensor_tensor(rest[:, :], weight[:, half, :], parts[:, 0, :], ALU.subtract).then_inc(sem_, n.step())
                v.wait_ge(sem_, n.total())
                v.tensor_copy(parts[:, 1, :], rest[:, :]).then_inc(sem_, n.step())
                v.wait_ge(sem_, n.total())
                v.tensor_tensor(parts[:, 2, :], rest[:, :], parts[:, 1, :], ALU.subtract).then_inc(sem_, n.step())
                assert n.steps == per

            def prep_chunk(batch, stage, i):
                def done(k):
                    v.wait_ge(prep_mm, prep_count(batch, stage, i, k) + 1)

                if stage == 1:
                    v.wait_ge(prep_x_loaded, 16 * (NC * batch + i + 1))
                    layernorm(NC * batch + i, prep_ln)
                    for half in range(HALVES):
                        done(half)
                        v.tensor_copy(h_t[:, half, bass.ds(i * CHUNK, CHUNK)], ps_step[:, :]).then_inc(prep_free, 1)
                if stage in (1, 2):
                    first = 2 if stage == 1 else 0
                    v.wait_ge(squared, weight_count(batch, stage, i))
                    for half in range(HALVES):
                        done(first + half)
                        v.tensor_copy(qk[:, half, :], ps_step[:, :]).then_inc(prep_free, 1)
                        v.wait_ge(prep_free, prep_count(batch, stage, i, first + half) + 1)
                        v.tensor_tensor(qk_sq[:, half, :], qk[:, half, :], qk[:, half, :], ALU.mult).then_inc(squared, 1)
                    v.wait_ge(q_split if stage == 1 else k_split, (4 if stage == 1 else 5) * 2 * (NC * batch + i))
                    for half in range(HALVES):
                        done(first + HALVES + half)
                        v.tensor_scalar(weight[:, half, :], ps_step[:, :], cen_sq[:, half:half + 1], 0.0,
                                        ALU.add, ALU.max).then_inc(prep_free, 1)
                    for half in range(HALVES):
                        split(batch, stage, i, half)
                if stage == 3:
                    v.wait_ge(vals_staged, NC * STAGES * batch)
                    for pair in range(2):
                        done(pair)
                        v.tensor_copy(v_all[:, bass.ds(i * TT + 2 * pair, 2), :],
                                      ps_step[:, :].rearrange("p (n d) -> p n d", d=D)).then_inc(prep_free, 1)

            def ffn_chunk(batch, i):
                nth = NC * batch + i

                def done(k):
                    v.wait_ge(ffn_mm, ffn_count(batch, i, k) + 1)

                v.wait_ge(ffn_x_loaded, 16 * (nth + 1))
                for pair in range(2):
                    rows = xin[:, 2 * pair:2 * pair + 2, :]
                    done(pair)
                    v.tensor_tensor(rows, ps_step[:, :].rearrange("p (n d) -> p n d", d=D), rows,
                                    ALU.add).then_inc(ffn_free, 1)
                v.wait_ge(ffn_free, ffn_count(batch, i, 2))
                layernorm(nth, ffn_ln)
                n = Count(9 * nth)
                v.wait_ge(mix_steps, n.total())
                v.tensor_copy(h2_t[:, :, 0:1], h2_t[:, :, CHUNK:CHUNK + 1]).then_inc(mix_steps, n.step())
                v.wait_ge(mix_steps, n.total())
                for half in range(HALVES):
                    done(2 + half)
                    v.tensor_copy(h2_t[:, half, 1:1 + CHUNK], ps_step[:, :]).then_inc(ffn_free, 1)
                v.wait_ge(ffn_free, ffn_count(batch, i, 4))
                for which, dst in ((1, mixed_k), (0, mixed_r)):
                    for half in range(HALVES):
                        v.wait_ge(mix_steps, n.total())
                        v.tensor_scalar(tmp[:, :], h2_t[:, half, 0:CHUNK], one_minus_mu[:, which, half:half + 1], None,
                                        ALU.mult).then_inc(mix_steps, n.step())
                        v.wait_ge(mix_steps, n.total())
                        v.scalar_tensor_tensor(out=dst[:, half, :], in0=h2_t[:, half, 1:1 + CHUNK],
                                               scalar=mu[:, which, half:half + 1], in1=tmp[:, :],
                                               op0=ALU.mult, op1=ALU.add).then_inc(mix_steps, n.step())
                assert n.steps == 9
                for half in range(HALVES):
                    done(4 + half)
                    v.wait_ge(act_steps, 2 * nth + half)
                    v.wait_ge(mix_steps, n.total())
                    v.tensor_scalar(tmp[:, :], ps_step[:, :], 0.0, None, ALU.max).then_inc(ffn_free, 1)
                    v.wait_ge(ffn_free, ffn_count(batch, i, 4 + half) + 1)
                    v.tensor_tensor(k_act[:, half, :], tmp[:, :], tmp[:, :], ALU.mult).then_inc(act_steps, 1)
                v.wait_ge(out_stored, 16 * nth)
                v.wait_ge(gate_steps, 3 * nth)
                for pair in range(2):
                    done(6 + pair)
                    v.tensor_scalar(gate_in[:, 2 * pair:2 * pair + 2, :],
                                    ps_step[:, :].rearrange("p (n d) -> p n d", d=D), -87.0, None,
                                    ALU.max).then_inc(ffn_free, 1)
                n = Count(3 * nth)
                v.wait_ge(gate_exp, 2 * (nth + 1))
                v.tensor_scalar(gate[:, :, :], gate[:, :, :], 1.0, None, ALU.add).then_inc(gate_steps, n.step())
                v.wait_ge(gate_steps, n.total())
                v.reciprocal(gate[:, :, :], gate[:, :, :]).then_inc(gate_steps, n.step())
                v.wait_ge(gate_steps, n.total())
                for pair in range(2):
                    done(8 + pair)
                    v.tensor_tensor(gate_in[:, 2 * pair:2 * pair + 2, :],
                                    ps_step[:, :].rearrange("p (n d) -> p n d", d=D), gate[:, 2 * pair:2 * pair + 2, :],
                                    ALU.mult).then_inc(ffn_free, 1)
                v.wait_ge(ffn_free, ffn_count(batch, i, FFN_STEPS))
                v.tensor_tensor(gate_in[:, :, :], gate_in[:, :, :], xin[:, :, :], ALU.add).then_inc(gate_steps, n.step())
                assert n.steps == 3

            def clear_carry(batch):
                v.memset(h2_t[:, :, CHUNK:CHUNK + 1], 0.0).then_inc(carry_cleared, 1)
                wait_alone(v, carry_cleared, batch + 1)

            def normalise(b, s, i):
                half, odd = s // 2, s % 2
                u = UNITS * b + NC * s + i
                n = Count(norm_count(b, s, i))
                dst = attn[:, half, bass.ds(i * CHUNK, CHUNK)]
                v.wait_ge(chunk_normed, u)
                v.wait_ge(pv_done, u + 1)
                v.tensor_copy(o_raw[:, :], ps_pv[:, :]).then_inc(pv_free, 1)
                wait_alone(v, pv_free, u + 1)
                v.stream_shuffle(den[:, :], o_raw[:, :], odd_den if odd else even_den).then_inc(norm_steps, n.step())
                v.wait_ge(norm_steps, n.total())
                v.reciprocal(den[:, :], den[:, :]).then_inc(norm_steps, n.step())
                v.wait_ge(norm_steps, n.total())
                if not odd:
                    v.tensor_tensor(dst, o_raw[:, :], den[:, :], ALU.mult).then_inc(chunk_normed, 1)
                else:
                    v.tensor_tensor(o_raw[:, :], o_raw[:, :], den[:, :], ALU.mult).then_inc(norm_steps, n.step())
                    v.wait_ge(norm_steps, n.total())
                    v.tensor_scalar(o_raw[:, :], o_raw[:, :], rowmask[:, 1:2], None, ALU.mult).then_inc(norm_steps, n.step())
                    v.wait_ge(norm_steps, n.total())
                    v.scalar_tensor_tensor(out=dst, in0=dst, scalar=rowmask[:, 0:1], in1=o_raw[:, :],
                                           op0=ALU.mult, op1=ALU.add).then_inc(chunk_normed, 1)

            def shift_pass(stage_no):
                with v.Fori(0, KT) as qt:
                    for c in range(HEADS_AT_ONCE):
                        v.wait_ge(max_free, MAX_STEPS * stage_no + HEADS_AT_ONCE * (NC + 1) * qt + (NC + 1) * c)
                        for kc in range(NC):
                            v.wait_ge(max_mm, MAX_TILES * stage_no + HEADS_AT_ONCE * NC * qt + NC * c + kc + 1)
                            v.tensor_reduce(tile_max[:, kc:kc + 1], ps_step[:, :], AX.X, ALU.max).then_inc(max_free, 1)
                        v.wait_ge(max_free, MAX_STEPS * stage_no + HEADS_AT_ONCE * (NC + 1) * qt + (NC + 1) * c + NC)
                        v.tensor_reduce(row_max[:, bass.ds(c * KT + qt, 1)], tile_max[:, :], AX.X, ALU.max,
                                        negate=True).then_inc(max_free, 1)
                v.wait_ge(max_mm, MAX_TILES * (stage_no + 1))
                v.tensor_copy(max_rows[:, :], ps_step[0:HEADS_AT_ONCE * KT, 0:P]).then_inc(max_free, 1)

            v.memset(vals[:, :, :, :, :], 1.0).then_inc(ones_set, 1)
            n = Count(0)

            def after():
                v.wait_ge(setup_dve, n.total())

            v.wait_ge(consts_loaded, 16 * N_CONSTS)
            v.wait_ge(setup_act, 3)
            v.tensor_scalar(params[:, 1:2], params[:, 1:2], 0.1, 10.0, ALU.max, ALU.min).then_inc(setup_dve, n.step())
            after()
            v.reciprocal(params[:, 1:2], params[:, 1:2]).then_inc(setup_dve, n.step())
            v.tensor_scalar(amp[:, :], amp[:, :], 1e-6, 10.0, ALU.max, ALU.min).then_inc(setup_dve, n.step())
            after()
            v.tensor_scalar(amp[:, :], amp[:, :], params[:, 1:2], None, ALU.mult).then_inc(setup_dve, n.step())
            after()
            assert n.steps == SETUP_AMP
            v.wait_ge(setup_pe, 1)
            v.tensor_copy(bound[:, :], ps_step[:, 0:HALVES]).then_inc(setup_dve, n.step())
            after()
            assert n.steps == SETUP_BOUND
            for half in range(HALVES):
                v.tensor_scalar(shift[:, half, :], bound[:, half:half + 1].broadcast_to([P, CHUNK]), -1.0, None,
                                ALU.mult).then_inc(setup_dve, n.step())
            assert n.steps == SETUP_SHIFT
            v.tensor_scalar(params[:, 0:1], params[:, 0:1], 1.0, None, ALU.add).then_inc(setup_dve, n.step())
            after()
            v.reciprocal(params[:, 0:1], params[:, 0:1]).then_inc(setup_dve, n.step())
            after()
            v.tensor_scalar(params[:, 0:1], params[:, 0:1], 0.2, None, ALU.mult).then_inc(setup_dve, n.step())
            after()
            for cen, dlt in ((cen_t, del_t), (cen_n, del_n)):
                v.scalar_tensor_tensor(out=cen[:, :, :], in0=dlt[:, :, :], scalar=params[:, 0:1], in1=cen[:, :, :],
                                       op0=ALU.mult, op1=ALU.add).then_inc(setup_dve, n.step())
            after()
            v.tensor_tensor(del_n[:, :, :], cen_n[:, :, :], cen_n[:, :, :], ALU.mult).then_inc(setup_dve, n.step())
            v.tensor_scalar(cen_t[:, :, :], cen_t[:, :, :], -2.0, None, ALU.mult).then_inc(setup_dve, n.step())
            after()
            v.tensor_reduce(cen_sq[:, :], del_n[:, :, :], AX.X, ALU.add).then_inc(setup_dve, n.step())
            for half in range(HALVES):
                v.tensor_tensor(cross[:, half, :].rearrange("p (h s) -> p h s", s=S),
                                headmask[:, :].rearrange("p (h s) -> p h s", s=S),
                                cen_t[:, half:half + 1, :].broadcast_to([P, P // S, S]),
                                ALU.mult).then_inc(setup_dve, n.step())
            v.tensor_scalar(inv_var[:, :], inv_var[:, :], 0.01, 2.0, ALU.max, ALU.min).then_inc(setup_dve, n.step())
            after()
            v.tensor_tensor(inv_var[:, :], inv_var[:, :], inv_var[:, :], ALU.mult).then_inc(setup_dve, n.step())
            after()
            v.tensor_scalar(inv_var[:, :], inv_var[:, :], 1e-8, None, ALU.add).then_inc(setup_dve, n.step())
            after()
            v.reciprocal(inv_var[:, :], inv_var[:, :]).then_inc(setup_dve, n.step())
            after()
            v.tensor_scalar(inv_var[:, :], inv_var[:, :], -0.5, None, ALU.mult).then_inc(setup_dve, n.step())
            v.tensor_scalar(one_minus_mu[:, :, :], mu[:, :, :], -1.0, 1.0, ALU.mult, ALU.add).then_inc(setup_dve, n.step())
            v.wait_ge(setup_pe, 2)
            v.tensor_reduce(flag_f[:, 0:1], ps_step[0:1, 0:HALVES * P], AX.X, ALU.max).then_inc(setup_dve, n.step())
            after()
            v.tensor_scalar(flag[:, :], flag_f[:, 0:1], SAFE_BOUND, None, ALU.is_gt).then_inc(setup_dve, n.step())
            after()
            assert n.steps == SETUP_STEPS, n.steps
            unsafe = v.value_load(flag[0:1, 0:1], min_val=0, max_val=1)

            for stage in (1, 2, 3):
                with v.Fori(0, NC) as i:
                    prep_chunk(0, stage, i)
            with v.If(unsafe == 1):
                shift_pass(0)

            def body(b, prep, ffn):
                for s in range(STAGES):
                    if s == 0 and ffn:
                        clear_carry(b - 1)
                    with v.Fori(0, NC) as i:
                        if s < STAGES - 1 or prep:
                            with v.If(unsafe * i == NC - 1):
                                shift_pass(STAGES * b + s + 1)
                        if s == 0 and ffn:
                            ffn_chunk(b - 1, i)
                        if s > 0 and prep:
                            prep_chunk(b + 1, s, i)
                        normalise(b, s, i)

            batches(v, body)
            clear_carry(NB - 1)
            with v.Fori(0, NC) as i:
                ffn_chunk(NB - 1, i)


N_CONSTS = 18
SETUP_AMP = 4
SETUP_BOUND = 5
SETUP_SHIFT = 7
SETUP_STEPS = 25


def kernel(L0_attn_x, L0_attn_splat_centers, L0_attn_splat_deltas, L0_attn_splat_log_scales,
           L0_attn_splat_log_amplitudes, L0_attn_movement_scale, L0_attn_temperature, L0_attn_qkv_w,
           L0_attn_out_w, L0_ffn_W_r, L0_ffn_W_k, L0_ffn_W_v, L0_ffn_mu_r, L0_ffn_mu_k):
    import numpy as np
    import concourse.bacc as bacc
    from concourse.bass_utils import run_bass_kernel_spmd

    def laid(a, shape=None):
        a = np.asarray(a)
        return np.ascontiguousarray(a if shape is None else a.reshape(shape))

    heads, splats, hd = np.shape(L0_attn_splat_centers)
    x = laid(L0_attn_x)
    d = x.shape[2]

    def dims_first(a):
        return laid(np.transpose(np.asarray(a), (0, 2, 1)), (heads * hd, splats))

    def columns(a):
        return laid(laid(a, (-1, P)).T)

    row = np.arange(P)
    arrays = {
        "x": x,
        "qkv_wT": laid(np.asarray(L0_attn_qkv_w).T),
        "out_wT": laid(np.asarray(L0_attn_out_w).T),
        "r_wT": laid(np.asarray(L0_ffn_W_r).T),
        "k_wT": laid(np.asarray(L0_ffn_W_k).T),
        "v_wT": laid(np.asarray(L0_ffn_W_v).T),
        "cen_hds": dims_first(L0_attn_splat_centers),
        "del_hds": dims_first(L0_attn_splat_deltas),
        "cen_hsd": laid(L0_attn_splat_centers, (heads * splats, hd)),
        "del_hsd": laid(L0_attn_splat_deltas, (heads * splats, hd)),
        "log_scales": columns(L0_attn_splat_log_scales),
        "log_amps": columns(L0_attn_splat_log_amplitudes),
        "movement": laid(L0_attn_movement_scale, (1, 1)),
        "temperature": laid(L0_attn_temperature, (1, 1)),
        "mu_r": columns(L0_ffn_mu_r),
        "mu_k": columns(L0_ffn_mu_k),
        "ident_in": np.eye(P, dtype=np.float32),
        "headmask_in": (row[:, None] // hd == row[None, :] // hd).astype(np.float32),
        "rowmask_in": np.stack([row // hd % 2 == 0, row // hd % 2 == 1], axis=1).astype(np.float32),
    }
    nc = bacc.Bacc("TRN2", target_bir_lowering=False, num_devices=1)
    args = [nc.dram_tensor(name, a.shape, mybir.dt.from_np(a.dtype), kind="ExternalInput").ap()
            for name, a in arrays.items()]
    out = nc.dram_tensor("out", x.shape, F32, kind="ExternalOutput").ap()
    preln_block(nc, *args, out)
    result = run_bass_kernel_spmd(nc, [arrays], core_ids=[0])
    return result.results[0]["out"]
```

```python
from contextlib import ExitStack

import concourse.bass as bass
from concourse import mybir

ALU = mybir.AluOpType
ACT = mybir.ActivationFunctionType
AX = mybir.AxisListType
F32 = mybir.dt.float32
BF16 = mybir.dt.bfloat16
I32 = mybir.dt.int32

P = 128
HEADS_AT_ONCE = 4
CHUNK = 512
BANKS_PER_GROUP = 3
PROB_SLOTS = 3
SAFE_BOUND = 60.0
LN_EPS = 1e-5
RSQRT_SEED = 0x5F3759DF
NEWTON = 3
LN_STEPS = 4 + 4 + 3 + 4 * NEWTON + 4
Q_TERMS = [0, 0, 1, 1, 0, 2]
K_TERMS = [0, 1, 0, 1, 2, 0]
TERMS = len(Q_TERMS)


class Count:

    def __init__(self, before):
        self.before, self.steps = before, 0

    def step(self):
        self.steps += 1
        return 1

    def total(self):
        return self.before + self.steps


def groups_of(tiles):
    found, at = [], 0
    while at < tiles:
        n = 2 if at % 8 == 6 else BANKS_PER_GROUP
        found.append((at, n))
        at += n
    return found


def preln_block(nc, x, qkv_wT, out_wT, r_wT, k_wT, v_wT, cen_hds, del_hds, cen_hsd, del_hsd,
                log_scales, log_amps, movement, temperature, mu_r, mu_k, ident_in, headmask_in,
                rowmask_in, out):
    NB, T, D = x.shape
    S = cen_hds.shape[1]
    NC = T // CHUNK
    KT = T // P
    TT = CHUNK // P
    HALVES = D // P
    STAGES = 2 * HALVES
    UNITS = NC * STAGES
    TILES = KT * HEADS_AT_ONCE
    GROUPS = groups_of(TILES)
    NG = len(GROUPS)
    SHIFT_ROW = TERMS * S
    ROWS = SHIFT_ROW + 1
    LOADS = 16 * (2 * TERMS + NC)
    FIRST_LOADS = 16 * NC * (2 * TERMS + 1)
    assert NG % (2 * PROB_SLOTS) == 0 and S == 16 and NC == STAGES == 4

    SECTIONS = {
        "turn0": ([("turn", 0), ("turn", 1)], None),
        "first": ([("project", 0, 0), ("project", 1, 0), ("value", 0), ("value", 1),
                   ("distance", 0, 0), ("distance", 1, 0)], None),
        "late": ([("project", 0, 1), ("project", 1, 1), ("distance", 0, 1), ("distance", 1, 1)], [5, 7, 10, 12]),
        1: ([("turn", 0), ("turn", 1), ("project", 0, 0), ("project", 0, 1),
             ("distance", 0, 0), ("distance", 0, 1)], [9, 10, 12, 13, 15, 16]),
        2: ([("project", 1, 0), ("project", 1, 1), ("distance", 1, 0), ("distance", 1, 1)], [5, 7, 10, 12]),
        3: ([("value", 0), ("value", 1)], [5, 7]),
    }
    PREP_TOTAL = 12 * NC
    STEPS_BEFORE = {"turn0": 0, "first": 2 * NC, "late": 8 * NC, 1: 0, 2: 6 * NC, 3: 10 * NC}
    TILES_BEFORE = {"first": 0, "late": 2 * NC, 1: 0, 2: 2 * NC}
    FFN_STEPS = 10
    FFN_AT = [4, 5, 9, 10, 12, 13, 14, 15, 18, 19]
    ACT_BEHIND = 2
    MAX_TILES = KT * HEADS_AT_ONCE * NC + 1
    MAX_STEPS = KT * HEADS_AT_ONCE * (NC + 1) + 1

    x_rows = x.rearrange("b t d -> (b t) d")
    out_rows = out.rearrange("b t d -> (b t) d")

    with ExitStack() as ctx:
        def sb(name, shape, dt=F32):
            return ctx.enter_context(nc.sbuf_tensor(name, shape, dt))

        def sem(name):
            return ctx.enter_context(nc.semaphore(name))

        wqkv = sb("wqkv", [P, HALVES, 3 * D])
        wout = sb("wout", [P, HALVES, D])
        wr = sb("wr", [P, HALVES, D])
        wk = sb("wk", [P, HALVES, D])
        wv = sb("wv", [P, HALVES, D])
        ident = sb("ident", [P, P])
        headmask = sb("headmask", [P, P])
        rowmask = sb("rowmask", [P, 2])
        cen_t = sb("cen_t", [P, HALVES, S])
        del_t = sb("del_t", [P, HALVES, S])
        cen_n = sb("cen_n", [P, HALVES, S])
        del_n = sb("del_n", [P, HALVES, S])
        cross = sb("cross", [P, HALVES, P])
        cen_sq = sb("cen_sq", [P, HALVES])
        inv_var = sb("inv_var", [P, HALVES])
        amp = sb("amp", [P, HALVES])
        bound = sb("bound", [P, HALVES])
        params = sb("params", [P, 2])
        mu = sb("mu", [P, 2, HALVES])
        one_minus_mu = sb("one_minus_mu", [P, 2, HALVES])
        flag_f = sb("flag_f", [1, 2])
        flag = sb("flag", [1, 1], I32)
        shift = sb("shift", [P, HALVES, CHUNK], BF16)
        k_aug = sb("k_aug", [ROWS, 2, HEADS_AT_ONCE, T], BF16)
        q_aug = sb("q_aug", [ROWS, 2, HEADS_AT_ONCE, T], BF16)
        vals = sb("vals", [P, 2, KT, HEADS_AT_ONCE, 32])
        probs = sb("probs", [P, PROB_SLOTS, BANKS_PER_GROUP, CHUNK])
        o_raw = sb("o_raw", [P, CHUNK])
        attn = sb("attn", [P, HALVES, T])
        staged = sb("staged", [P, HALVES, CHUNK])
        xin = sb("xin", [P, TT, D])
        h = sb("h", [P, TT, D])
        stats = sb("stats", [P, TT, 6])
        moments = sb("moments", [P, TT, 2])
        ln_v = sb("ln_v", [P, TT])
        ln_y = sb("ln_y", [P, TT])
        ln_a = sb("ln_a", [P, TT])
        h_t = sb("h_t", [P, HALVES, T])
        v_all = sb("v_all", [P, KT, D])
        qk = sb("qk", [P, HALVES, CHUNK])
        qk_sq = sb("qk_sq", [P, HALVES, CHUNK])
        weight = sb("weight", [P, HALVES, CHUNK])
        tmp = sb("tmp", [P, CHUNK])
        rest = den = tmp
        parts = sb("parts", [P, 3, CHUNK], BF16)
        h2_t = sb("h2_t", [P, HALVES, 1 + CHUNK])
        mixed_r, mixed_k = qk, qk_sq
        k_act = sb("k_act", [P, HALVES, CHUNK])
        gate_in = h
        gate = weight[:, :, :].rearrange("p a (n d) -> p (a n) d", d=D)
        tile_max = sb("tile_max", [P, NC])
        row_max = sb("row_max", [P, HEADS_AT_ONCE * KT])
        max_rows = sb("max_rows", [HEADS_AT_ONCE * KT, P], BF16)

        ps_scores = ctx.enter_context(nc.psum_tensor("ps_scores", [P, 2, BANKS_PER_GROUP, CHUNK], F32))
        ps_pv = ctx.enter_context(nc.psum_tensor("ps_pv", [P, CHUNK], F32))
        ps_step = ctx.enter_context(nc.psum_tensor("ps_step", [P, CHUNK], F32))

        q_parts = nc.dram_tensor("q_parts", [NB, 3, D, T], BF16, kind="Internal").ap()
        k_parts = nc.dram_tensor("k_parts", [NB, 3, D, T], BF16, kind="Internal").ap()

        consts_loaded = sem("consts_loaded")
        ones_set = sem("ones_set")
        setup_dve = sem("setup_dve")
        setup_act = sem("setup_act")
        setup_pe = sem("setup_pe")
        aug_loaded = sem("aug_loaded")
        scores_ready = sem("scores_ready")
        probs_ready = sem("probs_ready")
        pv_done = sem("pv_done")
        pv_free = sem("pv_free")
        vals_staged = sem("vals_staged")
        norm_steps = sem("norm_steps")
        chunk_normed = sem("chunk_normed")
        prep_x_loaded = sem("prep_x_loaded")
        prep_ln = sem("prep_ln")
        prep_mm = sem("prep_mm")
        prep_free = sem("prep_free")
        squared = sem("squared")
        weighted = sem("weighted")
        split_steps = sem("split_steps")
        parts_stored = sem("parts_stored")
        h_staged = sem("h_staged")
        ffn_x_loaded = sem("ffn_x_loaded")
        attn_staged = sem("attn_staged")
        ffn_ln = sem("ffn_ln")
        ffn_mm = sem("ffn_mm")
        ffn_free = sem("ffn_free")
        carry_cleared = sem("carry_cleared")
        mix_steps = sem("mix_steps")
        act_steps = sem("act_steps")
        gate_exp = sem("gate_exp")
        gate_steps = sem("gate_steps")
        out_stored = sem("out_stored")
        max_mm = sem("max_mm")
        max_free = sem("max_free")
        max_stored = sem("max_stored")

        counts = {id(eng): eng.alloc_register("waited_count") for eng in (nc.sync, nc.tensor, nc.vector, nc.gpsimd)}

        def wait_alone(eng, on, count):
            if not isinstance(count, int):
                eng.reg_mov(counts[id(eng)], count)
                count = counts[id(eng)]
            eng.wait_ge(consts_loaded, 16 * N_CONSTS)
            eng.wait_ge(on, count)

        def prep_count(batch, section, i, k=0):
            return PREP_TOTAL * batch + STEPS_BEFORE[section] + len(SECTIONS[section][0]) * i + k

        def tile_count(batch, section, i, nth=0):
            return 4 * NC * batch + TILES_BEFORE[section] + 2 * i + nth

        def loaded(stage_no):
            return FIRST_LOADS + LOADS * stage_no

        def ffn_count(batch, i, k=0):
            return FFN_STEPS * (NC * batch + i) + k

        NORM = (2, 4)

        def norm_count(b, s, i):
            return NC * (b * HALVES * sum(NORM) + s // 2 * sum(NORM) + s % 2 * NORM[0]) + NORM[s % 2] * i

        def prep_beside(b, s, prep, ffn):
            if s == 0:
                return None if ffn else (0, "late")
            return (b + 1, s) if prep else None

        def batches(eng, body):
            body(0, True, False)
            with eng.Fori(1, NB - 1) as b:
                body(b, True, True)
            body(NB - 1, False, True)

        block = ctx.enter_context(nc.Block())

        @block.sync
        def _(sp):
            consts = [
                (ident[:, :], ident_in), (headmask[:, :], headmask_in), (rowmask[:, :], rowmask_in),
                (params[:, 0:1], movement.broadcast_to([P, 1])),
                (params[:, 1:2], temperature.broadcast_to([P, 1])),
                (inv_var[:, :], log_scales),
                (amp[:, :], log_amps),
                (cen_t[:, :, :], cen_hds.rearrange("(a p) s -> p a s", p=P)),
                (del_t[:, :, :], del_hds.rearrange("(a p) s -> p a s", p=P)),
                (cen_n[:, :, :], cen_hsd.rearrange("(a p) s -> p a s", p=P)),
                (del_n[:, :, :], del_hsd.rearrange("(a p) s -> p a s", p=P)),
                (mu[:, 0, :], mu_r),
                (mu[:, 1, :], mu_k),
                (wqkv[:, :, :], qkv_wT.rearrange("(a p) n -> p a n", p=P)),
                (wout[:, :, :], out_wT.rearrange("(a p) n -> p a n", p=P)),
                (wr[:, :, :], r_wT.rearrange("(a p) n -> p a n", p=P)),
                (wk[:, :, :], k_wT.rearrange("(a p) n -> p a n", p=P)),
                (wv[:, :, :], v_wT.rearrange("(a p) n -> p a n", p=P)),
            ]
            assert len(consts) == N_CONSTS

            def load_x(batch, i, landed):
                rows = x_rows[bass.ds(batch * T + i * CHUNK, CHUNK), :]
                sp.dma_start(out=xin[:, :, :], in_=rows.rearrange("(n p) d -> p n d", p=P)).then_inc(landed, 16)

            def store_parts(batch, section, i):
                tiles = [step for step in SECTIONS[section][0] if step[0] == "distance"]
                for nth, (_, which, half) in enumerate(tiles):
                    wait_alone(sp, split_steps, 4 * (tile_count(batch, section, i, nth) + 1))
                    dram = (q_parts, k_parts)[which]
                    to = dram[bass.ds(batch, 1), :, half * P:(half + 1) * P, bass.ds(i * CHUNK, CHUNK)]
                    sp.dma_start(out=to.rearrange("o k p t -> p (o k) t"), in_=parts[:, :, :]).then_inc(parts_stored, 16)

            def load_aug(batch, stage, at, tokens):
                half, odd = stage // 2, stage % 2
                for dram, aug, terms in ((q_parts, q_aug, Q_TERMS), (k_parts, k_aug, K_TERMS)):
                    for j, part in enumerate(terms):
                        rows = dram[bass.ds(batch, 1), part, half * P:(half + 1) * P, bass.ds(at, tokens)]
                        rows = rows.rearrange("o (c e s) t -> (o s) c e t", e=2, s=S)[:, :, odd, :]
                        sp.dma_start(out=aug[j * S:(j + 1) * S, odd, :, bass.ds(at, tokens)], in_=rows).then_inc(aug_loaded, 16)
                for first in range(0, tokens, CHUNK):
                    sp.dma_start(out=q_aug[SHIFT_ROW:ROWS, odd, :, bass.ds(at + first, CHUNK)],
                                 in_=shift[odd * S:P:2 * S, half, :]).then_inc(aug_loaded, 16)

            def prep_dmas(batch, section, i):
                if section in ("turn0", 1):
                    sp.wait_ge(prep_ln, LN_STEPS * (NC * batch + i))
                    load_x(batch, i, prep_x_loaded)
                if section in ("first", "late", 1, 2):
                    store_parts(batch, section, i)

            def ffn_dmas(batch, i):
                sp.wait_ge(gate_steps, 3 * (NC * batch + i))
                load_x(batch, i, ffn_x_loaded)
                sp.wait_ge(gate_steps, 3 * (NC * batch + i + 1))
                rows = out_rows[bass.ds(batch * T + i * CHUNK, CHUNK), :]
                sp.dma_start(out=rows.rearrange("(n p) d -> p n d", p=P), in_=gate_in[:, :, :]).then_inc(out_stored, 16)

            with sp.Fori(0, 1) as i:
                load_x(0, i, prep_x_loaded)
            for to, of in consts:
                sp.dma_start(out=to, in_=of).then_inc(consts_loaded, 16)
            with sp.Fori(1, NC) as i:
                prep_dmas(0, "turn0", i)
            sp.wait_ge(setup_dve, SETUP_SHIFT)
            with sp.Fori(0, NC) as i:
                prep_dmas(0, "first", i)
                wait_alone(sp, parts_stored, 16 * tile_count(0, "first", i + 1))
                load_aug(0, 0, i * CHUNK, CHUNK)

            def body(b, prep, ffn):
                for s in range(STAGES):
                    if s < STAGES - 1 or prep:
                        nb, ns = (b, s + 1) if s < STAGES - 1 else (b + 1, 0)
                        wait_alone(sp, aug_loaded, loaded(STAGES * b + s))
                        if s > 0 or ffn:
                            sp.wait_ge(probs_ready, NG * NC * (STAGES * b + s))
                        if s == STAGES - 1:
                            wait_alone(sp, parts_stored, 16 * 4 * NC * (nb + 1))
                        if s == 1 and not ffn:
                            wait_alone(sp, parts_stored, 16 * 4 * NC)
                        load_aug(nb, ns, 0, T)
                    if s == 0 and not ffn:
                        with sp.Fori(0, NC) as i:
                            prep_dmas(0, "late", i)
                    if (s == 0 and ffn) or (s in (1, 2) and prep):
                        with sp.Fori(0, NC) as i:
                            if s == 0:
                                ffn_dmas(b - 1, i)
                            else:
                                if s == 1 and ffn:
                                    sp.wait_ge(gate_steps, 3 * NC * b)
                                prep_dmas(b + 1, s, i)

            batches(sp, body)
            with sp.Fori(0, NC) as i:
                ffn_dmas(NB - 1, i)
            sp.wait_ge(out_stored, 16 * NC * NB)

        @block.tensor
        def _(pe):
            def scores(g, par, query, last_inc=True):
                first, n = GROUPS[g]
                for m in range(n):
                    kt, c = divmod(first + m, HEADS_AT_ONCE)
                    mm = pe.matmul(ps_scores[:, g % 2, m, :], k_aug[:, par, c, kt * P:(kt + 1) * P],
                                   q_aug[:, par, c, bass.ds(query, CHUNK)], start=True, stop=True)
                mm.then_inc(scores_ready, 1)

            def values(g, par):
                first, n = GROUPS[g]
                for m in range(n):
                    kt, c = divmod(first + m, HEADS_AT_ONCE)
                    mm = pe.matmul(ps_pv[32 * c:32 * c + 32, :], vals[:, par, kt, c, :], probs[:, g % PROB_SLOTS, m, :],
                                   start=(kt == 0), stop=(kt == KT - 1))
                if g == NG - 1:
                    mm.then_inc(pv_done, 1)

            def turn(src, half, bank):
                for n in range(TT):
                    mm = pe.transpose(bank[:, n * P:(n + 1) * P], src[:, n, half * P:(half + 1) * P], ident[:, :])
                return mm

            def rows_out(lhs, w, pair, cols, bank):
                for m in range(2):
                    n = 2 * pair + m
                    for half in range(HALVES):
                        mm = pe.matmul(bank[:, m * D:(m + 1) * D], lhs[:, half, n * P:(n + 1) * P],
                                       w[:, half, cols:cols + D], start=(half == 0), stop=(half == HALVES - 1))
                return mm

            def prep_step(batch, section, i, k):
                steps = SECTIONS[section][0]
                kind, *which = steps[k]
                if section == "first":
                    bank = ps_scores[:, k // BANKS_PER_GROUP, k % BANKS_PER_GROUP, :]
                    pe.wait_ge(prep_free, prep_count(batch, section, i))
                else:
                    bank = ps_step[:, :]
                    pe.wait_ge(prep_free, prep_count(batch, section, i, k))
                if kind == "turn":
                    if which[0] == 0:
                        pe.wait_ge(prep_ln, LN_STEPS * (NC * batch + i + 1))
                    mm = turn(h, which[0], bank)
                elif kind == "value":
                    if which[0] == 0:
                        pe.wait_ge(h_staged, NC * batch + i + 1)
                    mm = rows_out(staged, wqkv, which[0], 2 * D, bank)
                elif kind == "project":
                    first = which[0] * D + which[1] * P
                    for half in range(HALVES):
                        mm = pe.matmul(bank, wqkv[:, half, first:first + P], h_t[:, half, bass.ds(i * CHUNK, CHUNK)],
                                       start=(half == 0), stop=(half == HALVES - 1))
                else:
                    nth = k - steps.index(next(x for x in steps if x[0] == "distance"))
                    pe.wait_ge(squared, tile_count(batch, section, i, nth) + 1)
                    pe.matmul(bank, headmask[:, :], qk_sq[:, nth, :], start=True, stop=False)
                    mm = pe.matmul(bank, cross[:, which[1], :], qk[:, nth, :], start=False, stop=True)
                mm.then_inc(prep_mm, 1)

            def ffn_step(batch, i, k):
                pe.wait_ge(ffn_free, ffn_count(batch, i, k))
                if k < 2:
                    if k == 0:
                        pe.wait_ge(attn_staged, NC * batch + i + 1)
                    mm = rows_out(staged, wout, k, 0, ps_step)
                elif k < 4:
                    if k == 2:
                        pe.wait_ge(ffn_ln, LN_STEPS * (NC * batch + i + 1))
                    mm = turn(h, k - 2, ps_step)
                elif k < 6:
                    if k == 4:
                        pe.wait_ge(mix_steps, 9 * (NC * batch + i) + 5)
                    mm = rows_out(mixed_r, wr, k - 4, 0, ps_step)
                elif k < 8:
                    if k == 6:
                        pe.wait_ge(mix_steps, 9 * (NC * batch + i + 1))
                    for half in range(HALVES):
                        mm = pe.matmul(ps_step[:, :], wk[:, half, (k - 6) * P:(k - 5) * P], mixed_k[:, half, :],
                                       start=(half == 0), stop=(half == 1))
                else:
                    if k == 8:
                        pe.wait_ge(act_steps, 2 * (NC * batch + i + 1))
                    mm = rows_out(k_act, wv, k - 8, 0, ps_step)
                mm.then_inc(ffn_mm, 1)

            def shift_pass(stage_no, par):
                with pe.Fori(0, KT) as qt:
                    for n in range(HEADS_AT_ONCE * NC):
                        c, kc = divmod(n, NC)
                        pe.wait_ge(max_free, MAX_STEPS * stage_no + HEADS_AT_ONCE * (NC + 1) * qt + (NC + 1) * c + kc)
                        pe.matmul(ps_step[:, :], q_aug[0:SHIFT_ROW, par, c, bass.ds(qt * P, P)],
                                  k_aug[0:SHIFT_ROW, par, c, kc * CHUNK:(kc + 1) * CHUNK], start=True, stop=True
                                  ).then_inc(max_mm, 1)
                wait_alone(pe, max_free, MAX_STEPS * (stage_no + 1) - 1)
                pe.transpose(ps_step[0:HEADS_AT_ONCE * KT, 0:P], row_max[:, :], ident[:, :]).then_inc(max_mm, 1)
                pe.wait_ge(max_free, MAX_STEPS * (stage_no + 1))
                pe.wait_ge(max_stored, 16 * (stage_no + 1))

            pe.wait_ge(consts_loaded, 16 * N_CONSTS)
            pe.wait_ge(setup_dve, SETUP_AMP)
            pe.matmul(ps_step[:, 0:HALVES], headmask[:, :], amp[:, :], start=True, stop=True).then_inc(setup_pe, 1)
            pe.wait_ge(setup_dve, SETUP_BOUND)
            for half in range(HALVES):
                mm = pe.matmul(ps_step[0:1, half * P:(half + 1) * P], bound[:, half:half + 1], ident[:, :],
                               start=True, stop=True)
            mm.then_inc(setup_pe, 1)
            pe.wait_ge(setup_dve, SETUP_STEPS)
            unsafe = pe.value_load(flag[0:1, 0:1], min_val=0, max_val=1)

            for section in ("turn0", "first"):
                with pe.Fori(0, NC) as i:
                    for k in range(len(SECTIONS[section][0])):
                        prep_step(0, section, i, k)

            pe.wait_ge(aug_loaded, loaded(0))
            pe.wait_ge(ones_set, 2)
            pe.wait_ge(prep_free, prep_count(0, "late", 0))
            with pe.If(unsafe == 1):
                shift_pass(0, 0)
            scores(0, 0, 0)
            scores(1, 0, 0)

            def unit(b, s, i, prep, ffn, finish=None, ends=False):
                par = s % 2
                last_stage = b == NB - 1 and s == STAGES - 1 if isinstance(b, int) else False
                if not last_stage:
                    with pe.If(unsafe * i == NC - 1):
                        pe.wait_ge(aug_loaded, loaded(STAGES * b + s + 1))
                        if finish:
                            wait_alone(pe, ffn_free, ffn_count(*finish))
                        elif prep:
                            wait_alone(pe, prep_free, prep_count(*prep, i))
                        shift_pass(STAGES * b + s + 1, 1 - par)
                u = UNITS * b + NC * s + i
                turn_over = 0 if last_stage else (i + 1) >> 2
                for g in range(NG):
                    pe.wait_ge(probs_ready, NG * u + g + 1)
                    if g + 2 < NG:
                        scores(g + 2, par, i * CHUNK)
                    elif not ends:
                        if g + 2 == NG and not last_stage:
                            wait_alone(pe, aug_loaded, loaded(STAGES * b + s + turn_over))
                        flip = turn_over if par == 0 else 1 - turn_over
                        scores_next(g + 2 - NG, flip, ((i + 1) & 3) * CHUNK)
                    if g == 0:
                        pe.wait_ge(pv_free, u)
                        pe.wait_ge(vals_staged, NC * (STAGES * b + s + 1))
                    values(g, par)
                    if finish and g in FFN_AT:
                        ffn_step(*finish, FFN_AT.index(g))
                    if prep and g in SECTIONS[prep[1]][1]:
                        prep_step(*prep, i, SECTIONS[prep[1]][1].index(g))

            def scores_next(g, par, query):
                first, n = GROUPS[g]
                for m in range(n):
                    kt, c = divmod(first + m, HEADS_AT_ONCE)
                    keys = k_aug[:, bass.ds(par, 1), c, kt * P:(kt + 1) * P].rearrange("r o t -> r (o t)")
                    queries = q_aug[:, bass.ds(par, 1), c, bass.ds(query, CHUNK)].rearrange("r o t -> r (o t)")
                    mm = pe.matmul(ps_scores[:, g % 2, m, :], keys, queries, start=True, stop=True)
                mm.then_inc(scores_ready, 1)

            def body(b, prep, ffn):
                for s in range(STAGES):
                    beside = prep_beside(b, s, prep, ffn)
                    if s == 0 and ffn:
                        wait_alone(pe, prep_free, PREP_TOTAL * (b + 1))
                    if s == 1 and ffn and prep:
                        wait_alone(pe, ffn_free, ffn_count(b, 0))
                    if s == STAGES - 1 and not prep:
                        unit(b, s, 0, None, ffn)
                        with pe.Fori(1, NC - 1) as i:
                            unit(b, s, i, None, ffn, finish=(b, i - 1))
                        unit(b, s, NC - 1, None, ffn, finish=(b, NC - 2), ends=True)
                    else:
                        with pe.Fori(0, NC) as i:
                            unit(b, s, i, beside, ffn, finish=(b - 1, i) if s == 0 and ffn else None)

            batches(pe, body)
            for k in range(FFN_STEPS):
                ffn_step(NB - 1, NC - 1, k)

        @block.scalar
        def _(act):
            def probabilities(b, s, i, g):
                n = GROUPS[g][1]
                act.wait_ge(scores_ready, NG * (UNITS * b + NC * s + i) + g + 1)
                act.activation(probs[:, g % PROB_SLOTS, 0:n, :], ps_scores[:, g % 2, 0:n, :], ACT.Exp).then_inc(probs_ready, 1)

            def prep_act(batch, section, i, k):
                steps = SECTIONS[section][0]
                kind, *which = steps[k]
                if kind in ("project", "distance"):
                    nth = k - steps.index(next(x for x in steps if x[0] == kind))
                    act.wait_ge(prep_free, prep_count(batch, section, i, k) + 1)
                    if kind == "project":
                        act.activation(qk_sq[:, nth, :], qk[:, nth, :], ACT.Square).then_inc(squared, 1)
                    else:
                        act.activation(weight[:, nth, :], weight[:, nth, :], ACT.Exp,
                                       scale=inv_var[:, which[1]:which[1] + 1]).then_inc(weighted, 1)

            def ffn_act(batch, i, k):
                if k in (4, 5):
                    pair = k - 4
                    act.wait_ge(ffn_free, ffn_count(batch, i, k) + 1)
                    act.activation(gate[:, 2 * pair:2 * pair + 2, :], gate_in[:, 2 * pair:2 * pair + 2, :],
                                   ACT.Exp, scale=-1.0).then_inc(gate_exp, 1)
                if k in (6, 7):
                    act.wait_ge(ffn_free, ffn_count(batch, i, k) + 1)
                    act.activation(k_act[:, k - 6, :], k_act[:, k - 6, :], ACT.Square).then_inc(act_steps, 1)

            act.wait_ge(consts_loaded, 16 * N_CONSTS)
            act.activation(params[:, 0:1], params[:, 0:1], ACT.Exp, scale=-1.0).then_inc(setup_act, 1)
            act.activation(inv_var[:, :], inv_var[:, :], ACT.Exp).then_inc(setup_act, 1)
            act.activation(amp[:, :], amp[:, :], ACT.Exp).then_inc(setup_act, 1)
            act.wait_ge(setup_dve, SETUP_STEPS)
            with act.Fori(0, NC) as i:
                for k in range(len(SECTIONS["first"][0])):
                    prep_act(0, "first", i, k)

            def unit(b, s, i, prep, finish=None):
                for g in range(NG):
                    probabilities(b, s, i, g)
                    if prep and g - ACT_BEHIND in SECTIONS[prep[1]][1]:
                        prep_act(*prep, i, SECTIONS[prep[1]][1].index(g - ACT_BEHIND))
                    if finish and g - ACT_BEHIND in FFN_AT:
                        ffn_act(*finish, FFN_AT.index(g - ACT_BEHIND))

            def body(b, prep, ffn):
                for s in range(STAGES):
                    if s == STAGES - 1 and not prep:
                        unit(b, s, 0, None)
                        with act.Fori(1, NC) as i:
                            unit(b, s, i, None, finish=(b, i - 1))
                    else:
                        with act.Fori(0, NC) as i:
                            unit(b, s, i, prep_beside(b, s, prep, ffn), finish=(b - 1, i) if s == 0 and ffn else None)

            batches(act, body)
            for k in range(FFN_STEPS):
                ffn_act(NB - 1, NC - 1, k)

        @block.gpsimd
        def _(pool):
            def stage_values(batch, stage, i):
                half, odd = stage // 2, stage % 2
                src = v_all[:, bass.ds(i * TT, TT), half * P:(half + 1) * P]
                src = src.rearrange("p k (c e d) -> p k c e d", e=2, d=16)
                for c in range(HEADS_AT_ONCE):
                    cp = pool.tensor_copy(vals[:, odd, bass.ds(i * TT, TT), c, 16 * odd:16 * odd + 16],
                                          src[:, :, c, odd, :])
                cp.then_inc(vals_staged, 1)

            def stage_h(batch, section, i):
                pool.wait_ge(prep_free, prep_count(batch, section, i))
                pool.tensor_copy(staged[:, :, :], h_t[:, :, bass.ds(i * CHUNK, CHUNK)]).then_inc(h_staged, 1)

            def values_written(batch, section, i):
                steps = SECTIONS[section][0]
                pool.wait_ge(prep_free, prep_count(batch, section, i, steps.index(("value", 1))) + 1)

            def stage_attn(batch, i):
                pool.wait_ge(ffn_mm, ffn_count(batch, i))
                pool.tensor_copy(staged[:, :, :], attn[:, :, bass.ds(i * CHUNK, CHUNK)]).then_inc(attn_staged, 1)

            def store_max(stage_no, par):
                wait_alone(pool, max_free, MAX_STEPS * (stage_no + 1))
                to = q_aug[SHIFT_ROW:ROWS, par, :, :].rearrange("o c (k t) -> o (c k) t", t=P)
                pool.dma_start(out=to, in_=max_rows[:, :]).then_inc(max_stored, 16)

            pool.memset(k_aug[SHIFT_ROW:ROWS, :, :, :], 1.0).then_inc(ones_set, 1)
            pool.wait_ge(setup_dve, SETUP_STEPS)
            unsafe = pool.value_load(flag[0:1, 0:1], min_val=0, max_val=1)
            pool.wait_ge(ones_set, 2)
            with pool.Fori(0, NC) as i:
                stage_h(0, "first", i)
                values_written(0, "first", i)
                stage_values(0, 0, i)
            with pool.If(unsafe == 1):
                store_max(0, 0)

            def body(b, prep, ffn):
                for s in range(STAGES):
                    par = s % 2
                    if s == STAGES - 1 and not prep:
                        with pool.Fori(0, NC) as i:
                            pool.wait_ge(chunk_normed, UNITS * b + NC * s + i + 1)
                            stage_attn(b, i)
                        continue
                    with pool.Fori(0, NC) as i:
                        with pool.If(unsafe * i == NC - 1):
                            store_max(STAGES * b + s + 1, 1 - par)
                        if s == 0 and ffn:
                            pool.wait_ge(chunk_normed, UNITS * b + i)
                            stage_attn(b - 1, i)
                        if s == STAGES - 1:
                            stage_h(b + 1, s, i)
                            values_written(b + 1, s, i)
                        if s > 0 or ffn:
                            pool.wait_ge(pv_done, UNITS * b + NC * s)
                        if s == STAGES - 1:
                            stage_values(b + 1, 0, i)
                        else:
                            stage_values(b, s + 1, i)

            batches(pool, body)

        @block.vector
        def _(v):
            even_den = [16 + i % 16 for i in range(32)]
            odd_den = [i % 16 for i in range(32)]

            def layernorm(nth, steps_sem):
                n = Count(LN_STEPS * nth)
                v.wait_ge(steps_sem, n.total())
                for t in range(TT):
                    v.bn_stats(out=stats[:, t, :], in_=xin[:, t, :]).then_inc(steps_sem, n.step())
                wait_alone(v, steps_sem, n.total())
                for t in range(TT):
                    v.bn_aggr(out=moments[:, t, :], in_=stats[:, t, :]).then_inc(steps_sem, n.step())
                v.wait_ge(steps_sem, n.total())
                v.tensor_scalar(ln_v[:, :], moments[:, :, 1], LN_EPS, None, ALU.add).then_inc(steps_sem, n.step())
                v.wait_ge(steps_sem, n.total())
                v.tensor_scalar(ln_a[:, :].bitcast(I32), ln_v[:, :].bitcast(I32), 1, None,
                                ALU.logical_shift_right).then_inc(steps_sem, n.step())
                v.wait_ge(steps_sem, n.total())
                v.tensor_scalar(ln_y[:, :].bitcast(I32), ln_a[:, :].bitcast(I32), -1.0, float(RSQRT_SEED),
                                ALU.mult, ALU.add).then_inc(steps_sem, n.step())
                for _ in range(NEWTON):
                    v.wait_ge(steps_sem, n.total())
                    v.tensor_tensor(ln_a[:, :], ln_y[:, :], ln_v[:, :], ALU.mult).then_inc(steps_sem, n.step())
                    v.wait_ge(steps_sem, n.total())
                    v.tensor_tensor(ln_a[:, :], ln_a[:, :], ln_y[:, :], ALU.mult).then_inc(steps_sem, n.step())
                    v.wait_ge(steps_sem, n.total())
                    v.tensor_scalar(ln_a[:, :], ln_a[:, :], -0.5, 1.5, ALU.mult, ALU.add).then_inc(steps_sem, n.step())
                    v.wait_ge(steps_sem, n.total())
                    v.tensor_tensor(ln_y[:, :], ln_y[:, :], ln_a[:, :], ALU.mult).then_inc(steps_sem, n.step())
                v.wait_ge(steps_sem, n.total())
                for t in range(TT):
                    v.tensor_scalar(h[:, t, :], xin[:, t, :], moments[:, t, 0:1], ln_y[:, t:t + 1],
                                    ALU.subtract, ALU.mult).then_inc(steps_sem, n.step())
                assert n.steps == LN_STEPS

            def split(batch, section, i, nth, which, half):
                n = Count(4 * tile_count(batch, section, i, nth))
                full = weight[:, nth, :]
                v.wait_ge(split_steps, n.total())
                v.wait_ge(weighted, tile_count(batch, section, i, nth) + 1)
                v.wait_ge(parts_stored, 16 * tile_count(batch, section, i, nth))
                if which:
                    scale = amp[:, half:half + 1]
                    v.tensor_scalar(parts[:, 0, :], full, scale, None, ALU.mult).then_inc(split_steps, n.step())
                    v.wait_ge(split_steps, n.total())
                    v.scalar_tensor_tensor(out=rest[:, :], in0=full, scalar=scale, in1=parts[:, 0, :],
                                           op0=ALU.mult, op1=ALU.subtract).then_inc(split_steps, n.step())
                else:
                    v.tensor_copy(parts[:, 0, :], full).then_inc(split_steps, n.step())
                    v.wait_ge(split_steps, n.total())
                    v.tensor_tensor(rest[:, :], full, parts[:, 0, :], ALU.subtract).then_inc(split_steps, n.step())
                v.wait_ge(split_steps, n.total())
                v.tensor_copy(parts[:, 1, :], rest[:, :]).then_inc(split_steps, n.step())
                v.wait_ge(split_steps, n.total())
                v.tensor_tensor(parts[:, 2, :], rest[:, :], parts[:, 1, :], ALU.subtract).then_inc(split_steps, n.step())
                assert n.steps == 4

            def prep_chunk(batch, section, i):
                steps = SECTIONS[section][0]
                if steps[0][0] == "turn":
                    v.wait_ge(prep_x_loaded, 16 * (NC * batch + i + 1))
                    layernorm(NC * batch + i, prep_ln)
                for k, (kind, *which) in enumerate(steps):
                    nth = k - steps.index(next(x for x in steps if x[0] == kind))
                    if section == "first":
                        bank = ps_scores[:, k // BANKS_PER_GROUP, k % BANKS_PER_GROUP, :]
                    else:
                        bank = ps_step[:, :]
                    if kind == "project" and nth == 0:
                        v.wait_ge(squared, tile_count(batch, section, i))
                    if kind == "distance" and nth == 0:
                        v.wait_ge(split_steps, 4 * tile_count(batch, section, i))
                    if kind == "value" and nth == 0:
                        v.wait_ge(vals_staged, NC * STAGES * batch)
                    v.wait_ge(prep_mm, prep_count(batch, section, i, k) + 1)
                    if kind == "turn":
                        v.tensor_copy(h_t[:, nth, bass.ds(i * CHUNK, CHUNK)], bank).then_inc(prep_free, 1)
                    elif kind == "project":
                        v.tensor_copy(qk[:, nth, :], bank).then_inc(prep_free, 1)
                    elif kind == "value":
                        v.tensor_copy(v_all[:, bass.ds(i * TT + 2 * nth, 2), :],
                                      bank.rearrange("p (n d) -> p n d", d=D)).then_inc(prep_free, 1)
                    else:
                        v.tensor_scalar(weight[:, nth, :], bank, cen_sq[:, which[1]:which[1] + 1], 0.0,
                                        ALU.add, ALU.max).then_inc(prep_free, 1)
                for nth, (_, which, half) in enumerate(x for x in steps if x[0] == "distance"):
                    split(batch, section, i, nth, which, half)

            def ffn_chunk(batch, i):
                nth = NC * batch + i

                def done(k):
                    v.wait_ge(ffn_mm, ffn_count(batch, i, k) + 1)

                v.wait_ge(ffn_x_loaded, 16 * (nth + 1))
                for pair in range(2):
                    rows = xin[:, 2 * pair:2 * pair + 2, :]
                    done(pair)
                    v.tensor_tensor(rows, ps_step[:, :].rearrange("p (n d) -> p n d", d=D), rows,
                                    ALU.add).then_inc(ffn_free, 1)
                v.wait_ge(ffn_free, ffn_count(batch, i, 2))
                v.wait_ge(out_stored, 16 * nth)
                layernorm(nth, ffn_ln)
                n = Count(9 * nth)
                v.wait_ge(mix_steps, n.total())
                v.tensor_copy(h2_t[:, :, 0:1], h2_t[:, :, CHUNK:CHUNK + 1]).then_inc(mix_steps, n.step())
                v.wait_ge(mix_steps, n.total())
                for half in range(HALVES):
                    done(2 + half)
                    v.tensor_copy(h2_t[:, half, 1:1 + CHUNK], ps_step[:, :]).then_inc(ffn_free, 1)
                v.wait_ge(ffn_free, ffn_count(batch, i, 4))
                for which, dst in ((0, mixed_r), (1, mixed_k)):
                    for half in range(HALVES):
                        v.wait_ge(mix_steps, n.total())
                        v.tensor_scalar(tmp[:, :], h2_t[:, half, 0:CHUNK], one_minus_mu[:, which, half:half + 1], None,
                                        ALU.mult).then_inc(mix_steps, n.step())
                        v.wait_ge(mix_steps, n.total())
                        v.scalar_tensor_tensor(out=dst[:, half, :], in0=h2_t[:, half, 1:1 + CHUNK],
                                               scalar=mu[:, which, half:half + 1], in1=tmp[:, :],
                                               op0=ALU.mult, op1=ALU.add).then_inc(mix_steps, n.step())
                assert n.steps == 9
                for pair in range(2):
                    done(4 + pair)
                    v.tensor_scalar(gate_in[:, 2 * pair:2 * pair + 2, :],
                                    ps_step[:, :].rearrange("p (n d) -> p n d", d=D), -87.0, None,
                                    ALU.max).then_inc(ffn_free, 1)
                for half in range(HALVES):
                    done(6 + half)
                    v.tensor_scalar(k_act[:, half, :], ps_step[:, :], 0.0, None, ALU.max).then_inc(ffn_free, 1)
                n = Count(3 * nth)
                v.wait_ge(gate_exp, 2 * (nth + 1))
                v.tensor_scalar(gate[:, :, :], gate[:, :, :], 1.0, None, ALU.add).then_inc(gate_steps, n.step())
                v.wait_ge(gate_steps, n.total())
                v.reciprocal(gate[:, :, :], gate[:, :, :]).then_inc(gate_steps, n.step())
                v.wait_ge(gate_steps, n.total())
                for pair in range(2):
                    done(8 + pair)
                    v.tensor_tensor(gate_in[:, 2 * pair:2 * pair + 2, :],
                                    ps_step[:, :].rearrange("p (n d) -> p n d", d=D), gate[:, 2 * pair:2 * pair + 2, :],
                                    ALU.mult).then_inc(ffn_free, 1)
                v.wait_ge(ffn_free, ffn_count(batch, i, FFN_STEPS))
                v.tensor_tensor(gate_in[:, :, :], gate_in[:, :, :], xin[:, :, :], ALU.add).then_inc(gate_steps, n.step())
                assert n.steps == 3

            def clear_carry(batch):
                v.memset(h2_t[:, :, CHUNK:CHUNK + 1], 0.0).then_inc(carry_cleared, 1)
                wait_alone(v, carry_cleared, batch + 1)

            def normalise(b, s, i):
                half, odd = s // 2, s % 2
                u = UNITS * b + NC * s + i
                n = Count(norm_count(b, s, i))
                dst = attn[:, half, bass.ds(i * CHUNK, CHUNK)]
                v.wait_ge(chunk_normed, u)
                v.wait_ge(pv_done, u + 1)
                v.tensor_copy(o_raw[:, :], ps_pv[:, :]).then_inc(pv_free, 1)
                wait_alone(v, pv_free, u + 1)
                v.stream_shuffle(den[:, :], o_raw[:, :], odd_den if odd else even_den).then_inc(norm_steps, n.step())
                v.wait_ge(norm_steps, n.total())
                v.reciprocal(den[:, :], den[:, :]).then_inc(norm_steps, n.step())
                v.wait_ge(norm_steps, n.total())
                if not odd:
                    v.tensor_tensor(dst, o_raw[:, :], den[:, :], ALU.mult).then_inc(chunk_normed, 1)
                else:
                    v.tensor_tensor(o_raw[:, :], o_raw[:, :], den[:, :], ALU.mult).then_inc(norm_steps, n.step())
                    v.wait_ge(norm_steps, n.total())
                    v.tensor_scalar(o_raw[:, :], o_raw[:, :], rowmask[:, 1:2], None, ALU.mult).then_inc(norm_steps, n.step())
                    v.wait_ge(norm_steps, n.total())
                    v.scalar_tensor_tensor(out=dst, in0=dst, scalar=rowmask[:, 0:1], in1=o_raw[:, :],
                                           op0=ALU.mult, op1=ALU.add).then_inc(chunk_normed, 1)

            def shift_pass(stage_no):
                with v.Fori(0, KT) as qt:
                    for c in range(HEADS_AT_ONCE):
                        v.wait_ge(max_free, MAX_STEPS * stage_no + HEADS_AT_ONCE * (NC + 1) * qt + (NC + 1) * c)
                        for kc in range(NC):
                            v.wait_ge(max_mm, MAX_TILES * stage_no + HEADS_AT_ONCE * NC * qt + NC * c + kc + 1)
                            v.tensor_reduce(tile_max[:, kc:kc + 1], ps_step[:, :], AX.X, ALU.max).then_inc(max_free, 1)
                        v.wait_ge(max_free, MAX_STEPS * stage_no + HEADS_AT_ONCE * (NC + 1) * qt + (NC + 1) * c + NC)
                        v.tensor_reduce(row_max[:, bass.ds(c * KT + qt, 1)], tile_max[:, :], AX.X, ALU.max,
                                        negate=True).then_inc(max_free, 1)
                v.wait_ge(max_mm, MAX_TILES * (stage_no + 1))
                v.tensor_copy(max_rows[:, :], ps_step[0:HEADS_AT_ONCE * KT, 0:P]).then_inc(max_free, 1)

            v.memset(vals[:, :, :, :, :], 1.0).then_inc(ones_set, 1)
            n = Count(0)

            def after():
                v.wait_ge(setup_dve, n.total())

            v.wait_ge(consts_loaded, 16 * N_CONSTS)
            v.wait_ge(setup_act, 3)
            v.tensor_scalar(params[:, 1:2], params[:, 1:2], 0.1, 10.0, ALU.max, ALU.min).then_inc(setup_dve, n.step())
            after()
            v.reciprocal(params[:, 1:2], params[:, 1:2]).then_inc(setup_dve, n.step())
            v.tensor_scalar(amp[:, :], amp[:, :], 1e-6, 10.0, ALU.max, ALU.min).then_inc(setup_dve, n.step())
            after()
            v.tensor_scalar(amp[:, :], amp[:, :], params[:, 1:2], None, ALU.mult).then_inc(setup_dve, n.step())
            after()
            assert n.steps == SETUP_AMP
            v.wait_ge(setup_pe, 1)
            v.tensor_copy(bound[:, :], ps_step[:, 0:HALVES]).then_inc(setup_dve, n.step())
            after()
            assert n.steps == SETUP_BOUND
            for half in range(HALVES):
                v.tensor_scalar(shift[:, half, :], bound[:, half:half + 1].broadcast_to([P, CHUNK]), -1.0, None,
                                ALU.mult).then_inc(setup_dve, n.step())
            assert n.steps == SETUP_SHIFT
            v.tensor_scalar(params[:, 0:1], params[:, 0:1], 1.0, None, ALU.add).then_inc(setup_dve, n.step())
            after()
            v.reciprocal(params[:, 0:1], params[:, 0:1]).then_inc(setup_dve, n.step())
            after()
            v.tensor_scalar(params[:, 0:1], params[:, 0:1], 0.2, None, ALU.mult).then_inc(setup_dve, n.step())
            after()
            for cen, dlt in ((cen_t, del_t), (cen_n, del_n)):
                v.scalar_tensor_tensor(out=cen[:, :, :], in0=dlt[:, :, :], scalar=params[:, 0:1], in1=cen[:, :, :],
                                       op0=ALU.mult, op1=ALU.add).then_inc(setup_dve, n.step())
            after()
            v.tensor_tensor(del_n[:, :, :], cen_n[:, :, :], cen_n[:, :, :], ALU.mult).then_inc(setup_dve, n.step())
            v.tensor_scalar(cen_t[:, :, :], cen_t[:, :, :], -2.0, None, ALU.mult).then_inc(setup_dve, n.step())
            after()
            v.tensor_reduce(cen_sq[:, :], del_n[:, :, :], AX.X, ALU.add).then_inc(setup_dve, n.step())
            for half in range(HALVES):
                v.tensor_tensor(cross[:, half, :].rearrange("p (h s) -> p h s", s=S),
                                headmask[:, :].rearrange("p (h s) -> p h s", s=S),
                                cen_t[:, half:half + 1, :].broadcast_to([P, P // S, S]),
                                ALU.mult).then_inc(setup_dve, n.step())
            v.tensor_scalar(inv_var[:, :], inv_var[:, :], 0.01, 2.0, ALU.max, ALU.min).then_inc(setup_dve, n.step())
            after()
            v.tensor_tensor(inv_var[:, :], inv_var[:, :], inv_var[:, :], ALU.mult).then_inc(setup_dve, n.step())
            after()
            v.tensor_scalar(inv_var[:, :], inv_var[:, :], 1e-8, None, ALU.add).then_inc(setup_dve, n.step())
            after()
            v.reciprocal(inv_var[:, :], inv_var[:, :]).then_inc(setup_dve, n.step())
            after()
            v.tensor_scalar(inv_var[:, :], inv_var[:, :], -0.5, None, ALU.mult).then_inc(setup_dve, n.step())
            v.tensor_scalar(one_minus_mu[:, :, :], mu[:, :, :], -1.0, 1.0, ALU.mult, ALU.add).then_inc(setup_dve, n.step())
            v.wait_ge(setup_pe, 2)
            v.tensor_reduce(flag_f[:, 0:1], ps_step[0:1, 0:HALVES * P], AX.X, ALU.max).then_inc(setup_dve, n.step())
            after()
            v.tensor_scalar(flag[:, :], flag_f[:, 0:1], SAFE_BOUND, None, ALU.is_gt).then_inc(setup_dve, n.step())
            after()
            assert n.steps == SETUP_STEPS, n.steps
            unsafe = v.value_load(flag[0:1, 0:1], min_val=0, max_val=1)

            for section in ("turn0", "first"):
                with v.Fori(0, NC) as i:
                    prep_chunk(0, section, i)
            with v.If(unsafe == 1):
                shift_pass(0)

            def unit(b, s, i, prep, finish=None, shifts=True):
                if shifts:
                    with v.If(unsafe * i == NC - 1):
                        shift_pass(STAGES * b + s + 1)
                if finish or prep:
                    v.wait_ge(chunk_normed, UNITS * b + NC * s + i)
                if finish:
                    ffn_chunk(*finish)
                if prep:
                    prep_chunk(*prep, i)
                    if prep[1] != 3:
                        v.wait_ge(split_steps, 4 * tile_count(*prep, i + 1))
                normalise(b, s, i)

            def body(b, prep, ffn):
                for s in range(STAGES):
                    if s == 0 and ffn:
                        clear_carry(b - 1)
                    if s == 1 and ffn and prep:
                        wait_alone(v, out_stored, 16 * NC * b)
                    if s == STAGES - 1 and not prep:
                        clear_carry(b)
                        unit(b, s, 0, None, shifts=False)
                        with v.Fori(1, NC) as i:
                            unit(b, s, i, None, finish=(b, i - 1), shifts=False)
                    else:
                        with v.Fori(0, NC) as i:
                            unit(b, s, i, prep_beside(b, s, prep, ffn), finish=(b - 1, i) if s == 0 and ffn else None)

            batches(v, body)
            v.wait_ge(chunk_normed, UNITS * NB)
            ffn_chunk(NB - 1, NC - 1)


N_CONSTS = 18
SETUP_AMP = 4
SETUP_BOUND = 5
SETUP_SHIFT = 7
SETUP_STEPS = 25


def kernel(L0_attn_x, L0_attn_splat_centers, L0_attn_splat_deltas, L0_attn_splat_log_scales,
           L0_attn_splat_log_amplitudes, L0_attn_movement_scale, L0_attn_temperature, L0_attn_qkv_w,
           L0_attn_out_w, L0_ffn_W_r, L0_ffn_W_k, L0_ffn_W_v, L0_ffn_mu_r, L0_ffn_mu_k):
    import numpy as np
    import concourse.bacc as bacc
    from concourse.bass_utils import run_bass_kernel_spmd

    def laid(a, shape=None):
        a = np.asarray(a)
        return np.ascontiguousarray(a if shape is None else a.reshape(shape))

    heads, splats, hd = np.shape(L0_attn_splat_centers)
    x = laid(L0_attn_x)
    d = x.shape[2]

    def dims_first(a):
        return laid(np.transpose(np.asarray(a), (0, 2, 1)), (heads * hd, splats))

    def columns(a):
        return laid(laid(a, (-1, P)).T)

    row = np.arange(P)
    arrays = {
        "x": x,
        "qkv_wT": laid(np.asarray(L0_attn_qkv_w).T),
        "out_wT": laid(np.asarray(L0_attn_out_w).T),
        "r_wT": laid(np.asarray(L0_ffn_W_r).T),
        "k_wT": laid(np.asarray(L0_ffn_W_k).T),
        "v_wT": laid(np.asarray(L0_ffn_W_v).T),
        "cen_hds": dims_first(L0_attn_splat_centers),
        "del_hds": dims_first(L0_attn_splat_deltas),
        "cen_hsd": laid(L0_attn_splat_centers, (heads * splats, hd)),
        "del_hsd": laid(L0_attn_splat_deltas, (heads * splats, hd)),
        "log_scales": columns(L0_attn_splat_log_scales),
        "log_amps": columns(L0_attn_splat_log_amplitudes),
        "movement": laid(L0_attn_movement_scale, (1, 1)),
        "temperature": laid(L0_attn_temperature, (1, 1)),
        "mu_r": columns(L0_ffn_mu_r),
        "mu_k": columns(L0_ffn_mu_k),
        "ident_in": np.eye(P, dtype=np.float32),
        "headmask_in": (row[:, None] // hd == row[None, :] // hd).astype(np.float32),
        "rowmask_in": np.stack([row // hd % 2 == 0, row // hd % 2 == 1], axis=1).astype(np.float32),
    }
    nc = bacc.Bacc("TRN2", target_bir_lowering=False, num_devices=1)
    args = [nc.dram_tensor(name, a.shape, mybir.dt.from_np(a.dtype), kind="ExternalInput").ap()
            for name, a in arrays.items()]
    out = nc.dram_tensor("out", x.shape, F32, kind="ExternalOutput").ap()
    preln_block(nc, *args, out)
    result = run_bass_kernel_spmd(nc, [arrays], core_ids=[0])
    return result.results[0]["out"]
```

```python
from contextlib import ExitStack

import concourse.bass as bass
from concourse import mybir

ALU = mybir.AluOpType
ACT = mybir.ActivationFunctionType
AX = mybir.AxisListType
F32 = mybir.dt.float32
BF16 = mybir.dt.bfloat16
I32 = mybir.dt.int32

P = 128
HEADS_AT_ONCE = 4
CHUNK = 512
BANKS_PER_GROUP = 2
AHEAD = 3
PROB_SLOTS = 2
SAFE_BOUND = 60.0
LN_EPS = 1e-5
RSQRT_SEED = 0x5F3759DF
NEWTON = 3
LN_STEPS = 4 + 4 + 3 + 4 * NEWTON + 4
TERM_BLOCKS = [(0, 3), (1, 2), (2, 1)]
TERMS = sum(n for _, n in TERM_BLOCKS)


class Count:

    def __init__(self, before):
        self.before, self.steps = before, 0

    def step(self):
        self.steps += 1
        return 1

    def total(self):
        return self.before + self.steps


def groups_of(tiles):
    found, at = [], 0
    while at < tiles:
        n = 1 if at < 2 else BANKS_PER_GROUP
        found.append((at, n))
        at += n
    return found


def preln_block(nc, x, qkv_wT, out_wT, r_wT, k_wT, v_wT, cen_hds, del_hds, cen_hsd, del_hsd,
                log_scales, log_amps, movement, temperature, mu_r, mu_k, ident_in, headmask_in,
                rowmask_in, out):
    NB, T, D = x.shape
    S = cen_hds.shape[1]
    NC = T // CHUNK
    KT = T // P
    TT = CHUNK // P
    HALVES = D // P
    STAGES = 2 * HALVES
    UNITS = NC * STAGES
    TILES = KT * HEADS_AT_ONCE
    GROUPS = groups_of(TILES)
    NG = len(GROUPS)
    SHIFT_ROW = TERMS * S
    ROWS = SHIFT_ROW + 1
    STORES = 16 * len(TERM_BLOCKS)
    LOADS = 16 * 3
    FIRST_LOADS = NC * LOADS
    assert NG == 2 * KT + 1 and NG % AHEAD == 0 and KT % PROB_SLOTS == 0 and S == 16 and NC == STAGES == 4

    SECTIONS = {
        "first": ([("project", 0, 0), ("project", 1, 0), ("value", 0), ("value", 1),
                   ("distance", 0, 0), ("distance", 1, 0)], None),
        "late": ([("project", 0, 1), ("project", 1, 1), ("distance", 0, 1), ("distance", 1, 1)], [-1, 7, 12, 16]),
        1: ([("turn", 0), ("turn", 1), ("project", 0, 0), ("project", 0, 1),
             ("distance", 0, 0), ("distance", 0, 1)], [13, 14, 16, 18, 20, 22]),
        2: ([("project", 1, 0), ("project", 1, 1), ("distance", 1, 0), ("distance", 1, 1)], [-1, 7, 12, 16]),
        3: ([("value", 0), ("value", 1)], [-1, 7]),
    }
    PREP_TOTAL = 12 * NC
    TURNS_APART = 2 * NC
    STEPS_BEFORE = {"first": 0, "late": 6 * NC, 1: 0 - TURNS_APART, 2: 6 * NC - TURNS_APART, 3: 10 * NC - TURNS_APART}
    TILES_BEFORE = {"first": 0, "late": 2 * NC, 1: 0, 2: 2 * NC}
    FFN_STEPS = 10
    WHOLE = dict(enumerate([-1, 4, 13, 14, 17, 19, 20, 22, 26, 29]))
    UPPER = dict(enumerate([-1, 6, 16, 18]))
    LOWER = dict(zip(range(4, FFN_STEPS), [-1, 6, 9, 12, 19, 22]))
    ACT_BEHIND = 6
    ACT_FIRST = 9
    MAX_TILES = KT * HEADS_AT_ONCE * NC + 1
    MAX_STEPS = KT * HEADS_AT_ONCE * (NC + 1) + 1

    x_rows = x.rearrange("b t d -> (b t) d")
    out_rows = out.rearrange("b t d -> (b t) d")

    with ExitStack() as ctx:
        def sb(name, shape, dt=F32):
            return ctx.enter_context(nc.sbuf_tensor(name, shape, dt))

        def sem(name):
            return ctx.enter_context(nc.semaphore(name))

        wqkv = sb("wqkv", [P, HALVES, 3 * D])
        wout = sb("wout", [P, HALVES, D])
        wr = sb("wr", [P, HALVES, D])
        wk = sb("wk", [P, HALVES, D])
        wv = sb("wv", [P, HALVES, D])
        ident = sb("ident", [P, P])
        headmask = sb("headmask", [P, P])
        rowmask = sb("rowmask", [P, 2])
        cen_t = sb("cen_t", [P, HALVES, S])
        del_t = sb("del_t", [P, HALVES, S])
        cen_n = sb("cen_n", [P, HALVES, S])
        del_n = sb("del_n", [P, HALVES, S])
        cross = sb("cross", [P, HALVES, P])
        cen_sq = sb("cen_sq", [P, HALVES])
        inv_var = sb("inv_var", [P, HALVES])
        amp = sb("amp", [P, HALVES])
        bound = sb("bound", [P, HALVES])
        params = sb("params", [P, 2])
        mu = sb("mu", [P, 2, HALVES])
        one_minus_mu = sb("one_minus_mu", [P, 2, HALVES])
        flag_f = sb("flag_f", [1, 2])
        flag = sb("flag", [1, 1], I32)
        shift = sb("shift", [P, HALVES, CHUNK], BF16)
        k_aug = sb("k_aug", [ROWS, 2, HEADS_AT_ONCE, T], BF16)
        q_aug = sb("q_aug", [ROWS, 2, HEADS_AT_ONCE, T], BF16)
        vals = sb("vals", [P, 2, KT, HEADS_AT_ONCE, 32])
        probs = sb("probs", [P, PROB_SLOTS, HEADS_AT_ONCE, CHUNK])
        o_raw = sb("o_raw", [P, CHUNK])
        attn = sb("attn", [P, HALVES, T])
        staged = sb("staged", [P, HALVES, CHUNK])
        x_prep = sb("x_prep", [P, TT, D])
        x_ffn = sb("x_ffn", [P, TT, D])
        h = sb("h", [P, TT, D])
        stats = sb("stats", [P, TT, 6])
        moments = sb("moments", [P, TT, 2])
        ln_v = sb("ln_v", [P, TT])
        ln_y = sb("ln_y", [P, TT])
        ln_a = sb("ln_a", [P, TT])
        h_t = sb("h_t", [P, HALVES, T])
        v_all = sb("v_all", [P, KT, D])
        qk = sb("qk", [P, HALVES, CHUNK])
        qk_sq = sb("qk_sq", [P, HALVES, CHUNK])
        weight = sb("weight", [P, HALVES, CHUNK])
        tmp = sb("tmp", [P, CHUNK])
        rest = den = tmp
        parts_first = sb("parts_first", [P, 3, CHUNK], BF16)
        h2_buffer = sb("h2_buffer", [P, HALVES * (1 + CHUNK)])
        h2_t = h2_buffer[:, :].rearrange("p (a t) -> p a t", a=HALVES)
        parts = [parts_first[:, :, :],
                 h2_buffer[:, 0:3 * CHUNK // 2].bitcast(BF16).rearrange("p (k t) -> p k t", k=3)]
        mixed_r, mixed_k = qk, qk_sq
        k_act = sb("k_act", [P, HALVES, CHUNK])
        gate_in = h
        gate = weight[:, :, :].rearrange("p a (n d) -> p (a n) d", d=D)
        tile_max = sb("tile_max", [P, NC])
        row_max = sb("row_max", [P, HEADS_AT_ONCE * KT])
        max_rows = sb("max_rows", [HEADS_AT_ONCE * KT, P], BF16)

        ps_scores = ctx.enter_context(nc.psum_tensor("ps_scores", [P, AHEAD, BANKS_PER_GROUP, CHUNK], F32))
        ps_pv = ctx.enter_context(nc.psum_tensor("ps_pv", [P, CHUNK], F32))
        ps_step = ctx.enter_context(nc.psum_tensor("ps_step", [P, CHUNK], F32))
        ps_setup = ps_scores[:, AHEAD - 1, BANKS_PER_GROUP - 1, :]

        q_parts = nc.dram_tensor("q_parts", [NB, D, TERMS, T], BF16, kind="Internal").ap()
        k_parts = nc.dram_tensor("k_parts", [NB, D, TERMS, T], BF16, kind="Internal").ap()

        consts_loaded = sem("consts_loaded")
        first_turned = sem("first_turned")
        first_copied = sem("first_copied")
        ones_set = sem("ones_set")
        setup_dve = sem("setup_dve")
        setup_act = sem("setup_act")
        setup_pe = sem("setup_pe")
        aug_loaded = sem("aug_loaded")
        scores_ready = sem("scores_ready")
        probs_ready = sem("probs_ready")
        pv_done = sem("pv_done")
        pv_free = sem("pv_free")
        vals_staged = sem("vals_staged")
        norm_steps = sem("norm_steps")
        chunk_normed = sem("chunk_normed")
        prep_x_loaded = sem("prep_x_loaded")
        prep_ln = sem("prep_ln")
        prep_mm = sem("prep_mm")
        prep_free = sem("prep_free")
        squared = sem("squared")
        weighted = sem("weighted")
        split_steps = sem("split_steps")
        parts_stored = [sem("parts_stored_first"), sem("parts_stored_second")]
        h_staged = sem("h_staged")
        ffn_x_loaded = sem("ffn_x_loaded")
        attn_staged = sem("attn_staged")
        ffn_ln = sem("ffn_ln")
        ffn_mm = sem("ffn_mm")
        ffn_free = sem("ffn_free")
        carry_cleared = sem("carry_cleared")
        mix_steps = sem("mix_steps")
        act_steps = sem("act_steps")
        gate_exp = sem("gate_exp")
        gate_steps = sem("gate_steps")
        out_stored = sem("out_stored")
        max_mm = sem("max_mm")
        max_free = sem("max_free")
        max_stored = sem("max_stored")

        waited_counts = {id(eng): eng.alloc_register("waited_count") for eng in (nc.sync, nc.tensor, nc.vector, nc.gpsimd)}

        def wait_alone(eng, on, count):
            if isinstance(count, int):
                eng.wait_ge(on, count)
                return
            eng.reg_mov(waited_counts[id(eng)], count)
            eng.wait_ge(consts_loaded, 16 * N_CONSTS)
            eng.wait_ge(on, waited_counts[id(eng)])

        def prep_count(batch, section, i, k=0):
            return PREP_TOTAL * batch + STEPS_BEFORE[section] + len(SECTIONS[section][0]) * i + k

        def tile_count(batch, section, i, nth=0):
            return 4 * NC * batch + TILES_BEFORE[section] + 2 * i + nth

        def loaded(stage_no):
            return FIRST_LOADS + LOADS * stage_no

        def ffn_count(batch, i, k=0):
            return FFN_STEPS * (NC * batch + i) + k

        def ffn_alone(batch, i):
            return isinstance(batch, int) and isinstance(i, int) and (batch, i) == (NB - 1, NC - 1)

        def ffn_bank(batch, i, k):
            if not ffn_alone(batch, i):
                return ps_step[:, :]
            bank = k % (AHEAD * BANKS_PER_GROUP)
            return ps_scores[:, bank // BANKS_PER_GROUP, bank % BANKS_PER_GROUP, :]

        NORM = (2, 4)

        def norm_count(b, s, i):
            return NC * (b * HALVES * sum(NORM) + s // 2 * sum(NORM) + s % 2 * NORM[0]) + NORM[s % 2] * i

        def prep_beside(b, s, prep, ffn):
            if s == 0:
                return None if ffn else (0, "late")
            return (b + 1, s) if prep else None

        def heads_of(batch):
            return h_t if isinstance(batch, int) and batch == NB - 1 else attn

        def batches(eng, body):
            body(0, True, False)
            with eng.Fori(1, NB - 1) as b:
                body(b, True, True)
            body(NB - 1, False, True)

        block = ctx.enter_context(nc.Block())

        @block.sync
        def _(sp):
            consts = [
                (ident[:, :], ident_in), (headmask[:, :], headmask_in), (rowmask[:, :], rowmask_in),
                (params[:, 0:1], movement.broadcast_to([P, 1])),
                (params[:, 1:2], temperature.broadcast_to([P, 1])),
                (inv_var[:, :], log_scales),
                (amp[:, :], log_amps),
                (cen_t[:, :, :], cen_hds.rearrange("(a p) s -> p a s", p=P)),
                (del_t[:, :, :], del_hds.rearrange("(a p) s -> p a s", p=P)),
                (cen_n[:, :, :], cen_hsd.rearrange("(a p) s -> p a s", p=P)),
                (del_n[:, :, :], del_hsd.rearrange("(a p) s -> p a s", p=P)),
                (mu[:, 0, :], mu_r),
                (mu[:, 1, :], mu_k),
                (wqkv[:, :, :], qkv_wT.rearrange("(a p) n -> p a n", p=P)),
                (wout[:, :, :], out_wT.rearrange("(a p) n -> p a n", p=P)),
                (wr[:, :, :], r_wT.rearrange("(a p) n -> p a n", p=P)),
                (wk[:, :, :], k_wT.rearrange("(a p) n -> p a n", p=P)),
                (wv[:, :, :], v_wT.rearrange("(a p) n -> p a n", p=P)),
            ]
            assert len(consts) == N_CONSTS

            def load_x(batch, i, xin, landed):
                rows = x_rows[bass.ds(batch * T + i * CHUNK, CHUNK), :]
                sp.dma_start(out=xin[:, :, :], in_=rows.rearrange("(n p) d -> p n d", p=P)).then_inc(landed, 16)

            def store_parts(batch, section, i):
                tiles = [step for step in SECTIONS[section][0] if step[0] == "distance"]
                for nth, (_, which, half) in enumerate(tiles):
                    wait_alone(sp, split_steps, 4 * (tile_count(batch, section, i, nth) + 1))
                    to = (q_parts, k_parts)[which][bass.ds(batch, 1), half * P:(half + 1) * P, :, bass.ds(i * CHUNK, CHUNK)]
                    to = to.rearrange("o p j t -> p (o j) t")
                    term = 0
                    for q_part, n in TERM_BLOCKS:
                        from_ = parts[nth][:, 0:n, :] if which else parts[nth][:, q_part:q_part + 1, :].broadcast_to([P, n, CHUNK])
                        sp.dma_start(out=to[:, term:term + n, :], in_=from_).then_inc(parts_stored[nth], 16)
                        term += n

            def load_aug(batch, stage, at, tokens):
                half, odd = stage // 2, stage % 2
                for dram, aug in ((q_parts, q_aug), (k_parts, k_aug)):
                    rows = dram[bass.ds(batch, 1), half * P:(half + 1) * P, :, bass.ds(at, tokens)]
                    rows = rows.rearrange("o (c e s) j t -> e (o s j) c t", e=2, s=S)[odd]
                    sp.dma_start(out=aug[0:SHIFT_ROW, odd, :, bass.ds(at, tokens)], in_=rows).then_inc(aug_loaded, 16)
                sp.dma_start(out=q_aug[SHIFT_ROW:ROWS, odd, :, bass.ds(at, tokens)],
                             in_=shift[odd * S:P:2 * S, half, :].unsqueeze(1).broadcast_to([HEADS_AT_ONCE, tokens // CHUNK, CHUNK])
                             ).then_inc(aug_loaded, 16)

            def load_prep_x(batch, i):
                sp.wait_ge(prep_ln, LN_STEPS * (NC * batch + i))
                load_x(batch, i, x_prep, prep_x_loaded)

            def load_ffn_x(batch, i):
                sp.wait_ge(gate_steps, 4 * (NC * batch + i))
                load_x(batch, i, x_ffn, ffn_x_loaded)

            def store_out(batch, i):
                sp.wait_ge(gate_steps, 4 * (NC * batch + i + 1))
                rows = out_rows[bass.ds(batch * T + i * CHUNK, CHUNK), :]
                sp.dma_start(out=rows.rearrange("(n p) d -> p n d", p=P), in_=gate_in[:, :, :]).then_inc(out_stored, 16)

            with sp.Fori(0, 1) as i:
                load_x(0, i, x_prep, prep_x_loaded)
            for to, of in consts:
                sp.dma_start(out=to, in_=of).then_inc(consts_loaded, 16)

            def first_parts(i, load_next):
                store_parts(0, "first", i)
                if load_next:
                    load_prep_x(0, i + 2)
                for stored in parts_stored:
                    wait_alone(sp, stored, STORES * (i + 1))
                load_aug(0, 0, i * CHUNK, CHUNK)

            load_prep_x(0, 1)
            sp.wait_ge(setup_dve, SETUP_SHIFT)
            with sp.Fori(0, NC - 2) as i:
                first_parts(i, True)
            with sp.Fori(NC - 2, NC) as i:
                first_parts(i, False)

            def body(b, prep, ffn):
                for s in range(STAGES):
                    if s == 0 and ffn:
                        load_ffn_x(b - 1, 0)
                    if s == 1 and not prep:
                        load_ffn_x(b - 1, NC // 2)
                    if s == 1 and prep:
                        load_prep_x(b + 1, 0)
                    if s < STAGES - 1 or prep:
                        nb, ns = (b, s + 1) if s < STAGES - 1 else (b + 1, 0)
                        wait_alone(sp, aug_loaded, loaded(STAGES * b + s))
                        if s > 0 or ffn:
                            sp.wait_ge(probs_ready, NG * NC * (STAGES * b + s))
                        if s == STAGES - 1:
                            for stored in parts_stored:
                                wait_alone(sp, stored, STORES * 2 * NC * (nb + 1))
                        if s == 1 and not ffn:
                            for stored in parts_stored:
                                wait_alone(sp, stored, STORES * 2 * NC)
                        load_aug(nb, ns, 0, T)
                    if s == 0 and not ffn:
                        with sp.Fori(0, NC) as i:
                            store_parts(0, "late", i)
                    if s == 0 and ffn and prep:
                        with sp.Fori(1, NC) as i:
                            store_out(b - 1, i - 1)
                            load_ffn_x(b - 1, i)
                        store_out(b - 1, NC - 1)
                    if s < 2 and not prep:
                        store_out(b - 1, NC // 2 * s)
                        load_ffn_x(b - 1, NC // 2 * s + 1)
                        store_out(b - 1, NC // 2 * s + 1)
                    if s == 1 and prep:
                        with sp.Fori(1, NC) as i:
                            load_prep_x(b + 1, i)
                            store_parts(b + 1, s, i - 1)
                        store_parts(b + 1, s, NC - 1)
                    if s == 2 and prep:
                        with sp.Fori(0, NC) as i:
                            store_parts(b + 1, s, i)

            batches(sp, body)
            with sp.Fori(0, NC) as i:
                load_ffn_x(NB - 1, i)
                store_out(NB - 1, i)
            sp.wait_ge(out_stored, 16 * NC * NB)

        @block.tensor
        def _(pe):
            def scores(g, par, query):
                first, n = GROUPS[g]
                for m in range(n):
                    kt, c = divmod(first + m, HEADS_AT_ONCE)
                    mm = pe.matmul(ps_scores[:, g % AHEAD, m, :], k_aug[:, par, c, kt * P:(kt + 1) * P],
                                   q_aug[:, par, c, bass.ds(query, CHUNK)], start=True, stop=True)
                mm.then_inc(scores_ready, 1)

            def values(kt, par):
                for c in range(HEADS_AT_ONCE):
                    mm = pe.matmul(ps_pv[32 * c:32 * c + 32, :], vals[:, par, kt, c, :], probs[:, kt % PROB_SLOTS, c, :],
                                   start=(kt == 0), stop=(kt == KT - 1))
                if kt == KT - 1:
                    mm.then_inc(pv_done, 1)

            def turn(src, half, bank):
                for n in range(TT):
                    mm = pe.transpose(bank[:, n * P:(n + 1) * P], src[:, n, half * P:(half + 1) * P], ident[:, :])
                return mm

            def rows_out(lhs, w, pair, cols, bank):
                for m in range(2):
                    n = 2 * pair + m
                    for half in range(HALVES):
                        mm = pe.matmul(bank[:, m * D:(m + 1) * D], lhs[:, half, n * P:(n + 1) * P],
                                       w[:, half, cols:cols + D], start=(half == 0), stop=(half == HALVES - 1))
                return mm

            def prep_step(batch, section, i, k):
                steps = SECTIONS[section][0]
                kind, *which = steps[k]
                if section == "first":
                    bank = ps_scores[:, k // BANKS_PER_GROUP, k % BANKS_PER_GROUP, :]
                    pe.wait_ge(prep_free, prep_count(batch, section, i))
                else:
                    bank = ps_step[:, :]
                    pe.wait_ge(prep_free, prep_count(batch, section, i, k))
                if kind == "turn":
                    if which[0] == 0:
                        pe.wait_ge(prep_ln, LN_STEPS * (NC * batch + i + 1))
                    mm = turn(h, which[0], bank)
                elif kind == "value":
                    if which[0] == 0:
                        pe.wait_ge(h_staged, NC * batch + i + 1)
                    mm = rows_out(staged, wqkv, which[0], 2 * D, bank)
                elif kind == "project":
                    first = which[0] * D + which[1] * P
                    for half in range(HALVES):
                        mm = pe.matmul(bank, wqkv[:, half, first:first + P], h_t[:, half, bass.ds(i * CHUNK, CHUNK)],
                                       start=(half == 0), stop=(half == HALVES - 1))
                else:
                    nth = k - steps.index(next(x for x in steps if x[0] == "distance"))
                    pe.wait_ge(squared, tile_count(batch, section, i, nth) + 1)
                    pe.matmul(bank, headmask[:, :], qk_sq[:, nth, :], start=True, stop=False)
                    mm = pe.matmul(bank, cross[:, which[1], :], qk[:, nth, :], start=False, stop=True)
                mm.then_inc(prep_mm, 1)

            def ffn_step(batch, i, k):
                bank = ffn_bank(batch, i, k)
                earlier = max(k + 1 - AHEAD * BANKS_PER_GROUP, 0) if ffn_alone(batch, i) else k
                pe.wait_ge(ffn_free, ffn_count(batch, i, earlier))
                if k < 2:
                    if k == 0:
                        pe.wait_ge(attn_staged, NC * batch + i + 1)
                    mm = rows_out(staged, wout, k, 0, bank)
                elif k < 4:
                    if k == 2:
                        pe.wait_ge(ffn_ln, LN_STEPS * (NC * batch + i + 1))
                    mm = turn(h, k - 2, bank)
                elif k < 6:
                    if k == 4:
                        pe.wait_ge(mix_steps, 9 * (NC * batch + i) + 5)
                    mm = rows_out(mixed_r, wr, k - 4, 0, bank)
                elif k < 8:
                    if k == 6:
                        pe.wait_ge(mix_steps, 9 * (NC * batch + i + 1))
                    for half in range(HALVES):
                        mm = pe.matmul(bank, wk[:, half, (k - 6) * P:(k - 5) * P], mixed_k[:, half, :],
                                       start=(half == 0), stop=(half == 1))
                else:
                    if k == 8:
                        pe.wait_ge(act_steps, 2 * (NC * batch + i + 1))
                    mm = rows_out(k_act, wv, k - 8, 0, bank)
                mm.then_inc(ffn_mm, 1)

            def shift_pass(stage_no, par):
                with pe.Fori(0, KT) as qt:
                    for n in range(HEADS_AT_ONCE * NC):
                        c, kc = divmod(n, NC)
                        pe.wait_ge(max_free, MAX_STEPS * stage_no + HEADS_AT_ONCE * (NC + 1) * qt + (NC + 1) * c + kc)
                        pe.matmul(ps_step[:, :], q_aug[0:SHIFT_ROW, par, c, bass.ds(qt * P, P)],
                                  k_aug[0:SHIFT_ROW, par, c, kc * CHUNK:(kc + 1) * CHUNK], start=True, stop=True
                                  ).then_inc(max_mm, 1)
                wait_alone(pe, max_free, MAX_STEPS * (stage_no + 1) - 1)
                pe.transpose(ps_step[0:HEADS_AT_ONCE * KT, 0:P], row_max[:, :], ident[:, :]).then_inc(max_mm, 1)
                pe.wait_ge(max_free, MAX_STEPS * (stage_no + 1))
                pe.wait_ge(max_stored, 16 * (stage_no + 1))

            def first_turns(i):
                pe.wait_ge(first_copied, HALVES * i)
                pe.wait_ge(prep_ln, LN_STEPS * (i + 1))
                for half, bank in ((0, ps_step[:, :]), (1, ps_pv[:, :])):
                    turn(h, half, bank).then_inc(first_turned, 1)

            def first_steps(i):
                pe.wait_ge(first_copied, HALVES * (i + 1))
                for k in range(len(SECTIONS["first"][0])):
                    prep_step(0, "first", i, k)

            pe.wait_ge(consts_loaded, 16 * N_CONSTS)
            first_turns(0)
            pe.wait_ge(setup_dve, SETUP_AMP)
            pe.matmul(ps_setup[:, 0:HALVES], headmask[:, :], amp[:, :], start=True, stop=True).then_inc(setup_pe, 1)
            pe.wait_ge(setup_dve, SETUP_BOUND)
            for half in range(HALVES):
                mm = pe.matmul(ps_setup[0:1, half * P:(half + 1) * P], bound[:, half:half + 1], ident[:, :],
                               start=True, stop=True)
            mm.then_inc(setup_pe, 1)
            pe.wait_ge(setup_dve, SETUP_STEPS)
            unsafe = pe.value_load(flag[0:1, 0:1], min_val=0, max_val=1)

            with pe.Fori(0, NC - 1) as i:
                first_steps(i)
                first_turns(i + 1)
            first_steps(NC - 1)

            pe.wait_ge(aug_loaded, loaded(0))
            pe.wait_ge(ones_set, 2)
            pe.wait_ge(prep_free, prep_count(0, "late", 0))
            with pe.If(unsafe == 1):
                shift_pass(0, 0)
            scores(0, 0, 0)
            scores(1, 0, 0)
            scores(2, 0, 0)
            pe.wait_ge(probs_ready, 1)
            scores(3, 0, 0)

            def unit(b, s, i, prep, ffn, finish=None, ends=False):
                par = s % 2
                last_stage = b == NB - 1 and s == STAGES - 1 if isinstance(b, int) else False
                if not last_stage:
                    with pe.If(unsafe * i == NC - 1):
                        pe.wait_ge(aug_loaded, loaded(STAGES * b + s + 1))
                        if finish:
                            wait_alone(pe, ffn_free, ffn_count(*finish[:2], min(finish[2])))
                        elif prep:
                            wait_alone(pe, prep_free, prep_count(*prep, i))
                        shift_pass(STAGES * b + s + 1, 1 - par)
                u = UNITS * b + NC * s + i
                turn_over = 0 if last_stage else (i + 1) >> 2

                def side_step(g):
                    if finish:
                        for k, at in finish[2].items():
                            if g == at:
                                ffn_step(*finish[:2], k)
                    if prep and g in SECTIONS[prep[1]][1]:
                        prep_step(*prep, i, SECTIONS[prep[1]][1].index(g))

                flip = turn_over if par == 0 else 1 - turn_over

                def scores_ahead(g):
                    if g < NG:
                        scores(g, par, i * CHUNK)
                    elif not ends:
                        scores_next(g - NG, flip, ((i + 1) & 3) * CHUNK)

                side_step(-1)
                for kt in range(KT):
                    pe.wait_ge(probs_ready, NG * u + 2 * kt + 3)
                    if kt == 0:
                        scores(4, par, i * CHUNK)
                        pe.wait_ge(pv_free, u)
                        pe.wait_ge(vals_staged, NC * (STAGES * b + s + 1))
                    values(kt, par)
                    if kt == KT - 2 and not last_stage:
                        wait_alone(pe, aug_loaded, loaded(STAGES * b + s + turn_over))
                    scores_ahead(2 * kt + 5)
                    side_step(2 * kt)
                    if not (ends and kt == KT - 1):
                        pe.wait_ge(probs_ready, NG * u + 2 * kt + 4)
                    scores_ahead(2 * kt + 6)
                    side_step(2 * kt + 1)

            def scores_next(g, par, query):
                first, n = GROUPS[g]
                for m in range(n):
                    kt, c = divmod(first + m, HEADS_AT_ONCE)
                    keys = k_aug[:, bass.ds(par, 1), c, kt * P:(kt + 1) * P].rearrange("r o t -> r (o t)")
                    queries = q_aug[:, bass.ds(par, 1), c, bass.ds(query, CHUNK)].rearrange("r o t -> r (o t)")
                    mm = pe.matmul(ps_scores[:, g % AHEAD, m, :], keys, queries, start=True, stop=True)
                mm.then_inc(scores_ready, 1)

            def body(b, prep, ffn):
                for s in range(STAGES):
                    beside = prep_beside(b, s, prep, ffn)
                    if s == 0 and ffn:
                        wait_alone(pe, prep_free, PREP_TOTAL * (b + 1) - TURNS_APART)
                    if s == 1 and ffn and prep:
                        wait_alone(pe, ffn_free, ffn_count(b, 0))
                    if s == STAGES - 1 and not prep:
                        unit(b, s, 0, None, ffn)
                        with pe.Fori(1, NC - 1) as i:
                            unit(b, s, i, None, ffn, finish=(b, i - 1, WHOLE))
                        unit(b, s, NC - 1, None, ffn, finish=(b, NC - 2, WHOLE), ends=True)
                    elif s < 2 and not prep:
                        with pe.Fori(0, NC // 2) as pair:
                            for n, steps in enumerate((UPPER, LOWER)):
                                unit(b, s, 2 * pair + n, None, ffn, finish=(b - 1, NC // 2 * s + pair, steps))
                    else:
                        with pe.Fori(0, NC) as i:
                            unit(b, s, i, beside, ffn, finish=(b - 1, i, WHOLE) if s == 0 and ffn else None)

            batches(pe, body)
            for k in range(FFN_STEPS):
                ffn_step(NB - 1, NC - 1, k)

        @block.scalar
        def _(act):
            def probabilities(b, s, i, g):
                first, n = GROUPS[g]
                kt, c = divmod(first, HEADS_AT_ONCE)
                act.wait_ge(scores_ready, NG * (UNITS * b + NC * s + i) + g + 1)
                act.activation(probs[:, kt % PROB_SLOTS, c:c + n, :], ps_scores[:, g % AHEAD, 0:n, :],
                               ACT.Exp).then_inc(probs_ready, 1)

            def prep_act(batch, section, i, k):
                steps = SECTIONS[section][0]
                kind, *which = steps[k]
                if kind in ("project", "distance"):
                    nth = k - steps.index(next(x for x in steps if x[0] == kind))
                    act.wait_ge(prep_free, prep_count(batch, section, i, k) + 1)
                    if kind == "project":
                        act.activation(qk_sq[:, nth, :], qk[:, nth, :], ACT.Square).then_inc(squared, 1)
                    else:
                        act.activation(weight[:, nth, :], weight[:, nth, :], ACT.Exp,
                                       scale=inv_var[:, which[1]:which[1] + 1]).then_inc(weighted, 1)

            def ffn_act(batch, i, k):
                if k in (4, 5):
                    pair = k - 4
                    act.wait_ge(ffn_free, ffn_count(batch, i, k) + 1)
                    act.activation(gate[:, 2 * pair:2 * pair + 2, :], gate_in[:, 2 * pair:2 * pair + 2, :],
                                   ACT.Exp, scale=-1.0).then_inc(gate_exp, 1)
                if k in (6, 7):
                    act.wait_ge(ffn_free, ffn_count(batch, i, k) + 1)
                    act.activation(k_act[:, k - 6, :], k_act[:, k - 6, :], ACT.Square).then_inc(act_steps, 1)

            def first_copies(i):
                for half, bank in ((0, ps_step[:, :]), (1, ps_pv[:, :])):
                    act.wait_ge(first_turned, HALVES * i + half + 1)
                    act.activation(h_t[:, half, bass.ds(i * CHUNK, CHUNK)], bank, ACT.Copy).then_inc(first_copied, 1)

            act.wait_ge(consts_loaded, 16 * N_CONSTS)
            act.activation(params[:, 0:1], params[:, 0:1], ACT.Exp, scale=-1.0).then_inc(setup_act, 1)
            act.activation(inv_var[:, :], inv_var[:, :], ACT.Exp).then_inc(setup_act, 1)
            act.activation(amp[:, :], amp[:, :], ACT.Exp).then_inc(setup_act, 1)
            with act.Fori(0, 1) as i:
                first_copies(i)
            act.wait_ge(setup_dve, SETUP_STEPS)
            with act.Fori(0, NC - 1) as i:
                for k in range(len(SECTIONS["first"][0])):
                    prep_act(0, "first", i, k)
                first_copies(i + 1)
            for k in range(len(SECTIONS["first"][0])):
                prep_act(0, "first", NC - 1, k)

            def unit(b, s, i, prep, finish=None):
                for g in range(NG):
                    probabilities(b, s, i, g)
                    if prep:
                        for k, at in enumerate(SECTIONS[prep[1]][1]):
                            if g == max(at + ACT_BEHIND, ACT_FIRST):
                                prep_act(*prep, i, k)
                    if finish:
                        for k, at in finish[2].items():
                            if g == min(max(at + ACT_BEHIND, ACT_FIRST), NG - 1):
                                ffn_act(*finish[:2], k)

            def body(b, prep, ffn):
                for s in range(STAGES):
                    if s == STAGES - 1 and not prep:
                        unit(b, s, 0, None)
                        with act.Fori(1, NC) as i:
                            unit(b, s, i, None, finish=(b, i - 1, WHOLE))
                    elif s < 2 and not prep:
                        with act.Fori(0, NC // 2) as pair:
                            for n, steps in enumerate((UPPER, LOWER)):
                                unit(b, s, 2 * pair + n, None, finish=(b - 1, NC // 2 * s + pair, steps))
                    else:
                        with act.Fori(0, NC) as i:
                            unit(b, s, i, prep_beside(b, s, prep, ffn), finish=(b - 1, i, WHOLE) if s == 0 and ffn else None)

            batches(act, body)
            act.wait_ge(chunk_normed, UNITS * NB)
            act.wait_ge(ffn_mm, ffn_count(NB - 1, NC - 2, 2))
            act.activation(staged[:, :, :], heads_of(NB - 1)[:, :, T - CHUNK:T], ACT.Copy).then_inc(attn_staged, 1)
            for k in range(FFN_STEPS):
                ffn_act(NB - 1, NC - 1, k)

        @block.gpsimd
        def _(pool):
            def stage_values(batch, stage, i):
                half, odd = stage // 2, stage % 2
                src = v_all[:, bass.ds(i * TT, TT), half * P:(half + 1) * P]
                src = src.rearrange("p k (c e d) -> p k c e d", e=2, d=16)
                for c in range(HEADS_AT_ONCE):
                    cp = pool.tensor_copy(vals[:, odd, bass.ds(i * TT, TT), c, 16 * odd:16 * odd + 16],
                                          src[:, :, c, odd, :])
                cp.then_inc(vals_staged, 1)

            def stage_h(batch, section, i):
                pool.wait_ge(prep_free, prep_count(batch, section, i))
                pool.tensor_copy(staged[:, :, :], h_t[:, :, bass.ds(i * CHUNK, CHUNK)]).then_inc(h_staged, 1)

            def values_written(batch, section, i):
                steps = SECTIONS[section][0]
                pool.wait_ge(prep_free, prep_count(batch, section, i, steps.index(("value", 1))) + 1)

            def stage_attn(batch, i, first=False):
                wait_alone(pool, ffn_mm, ffn_count(batch, i) if first else ffn_count(batch, i - 1, 2))
                pool.tensor_copy(staged[:, :, :], heads_of(batch)[:, :, bass.ds(i * CHUNK, CHUNK)]).then_inc(attn_staged, 1)

            def store_max(stage_no, par):
                wait_alone(pool, max_free, MAX_STEPS * (stage_no + 1))
                to = q_aug[SHIFT_ROW:ROWS, par, :, :].rearrange("o c (k t) -> o (c k) t", t=P)
                pool.dma_start(out=to, in_=max_rows[:, :]).then_inc(max_stored, 16)

            pool.memset(k_aug[SHIFT_ROW:ROWS, :, :, :], 1.0).then_inc(ones_set, 1)
            pool.wait_ge(setup_dve, SETUP_STEPS)
            unsafe = pool.value_load(flag[0:1, 0:1], min_val=0, max_val=1)
            pool.wait_ge(ones_set, 2)
            with pool.Fori(0, NC) as i:
                pool.wait_ge(first_copied, HALVES * (i + 1))
                stage_h(0, "first", i)
                values_written(0, "first", i)
                stage_values(0, 0, i)
            with pool.If(unsafe == 1):
                store_max(0, 0)

            def body(b, prep, ffn):
                for s in range(STAGES):
                    par = s % 2
                    if s == STAGES - 1 and not prep:
                        pool.wait_ge(chunk_normed, UNITS * b + NC * s + 1)
                        stage_attn(b, 0, first=True)
                        with pool.Fori(1, NC - 1) as i:
                            pool.wait_ge(chunk_normed, UNITS * b + NC * s + i + 1)
                            stage_attn(b, i)
                        continue

                    def beside_unit(i, first, chunk):
                        with pool.If(unsafe * i == NC - 1):
                            store_max(STAGES * b + s + 1, 1 - par)
                        if chunk is not None:
                            wait_alone(pool, chunk_normed, UNITS * b - (NC - 1) + chunk)
                            stage_attn(b - 1, chunk, first)
                        if s == STAGES - 1:
                            stage_h(b + 1, s, i)
                            values_written(b + 1, s, i)
                        if s > 0 or ffn:
                            wait_alone(pool, pv_done, UNITS * b + NC * s)
                        if s == STAGES - 1:
                            stage_values(b + 1, 0, i)
                        else:
                            stage_values(b, s + 1, i)

                    if s < 2 and not prep:
                        with pool.Fori(0, NC // 2) as pair:
                            beside_unit(2 * pair, False, NC // 2 * s + pair)
                            beside_unit(2 * pair + 1, False, None)
                        continue
                    staging = s == 0 and ffn
                    if staging:
                        with pool.Fori(0, 1) as i:
                            beside_unit(i, True, i)
                    with pool.Fori(1 if staging else 0, NC) as i:
                        beside_unit(i, False, i if staging else None)

            batches(pool, body)

        @block.vector
        def _(v):
            even_den = [16 + i % 16 for i in range(32)]
            odd_den = [i % 16 for i in range(32)]

            def layernorm(nth, xin, steps_sem):
                n = Count(LN_STEPS * nth)
                v.wait_ge(steps_sem, n.total())
                for t in range(TT):
                    v.bn_stats(out=stats[:, t, :], in_=xin[:, t, :]).then_inc(steps_sem, n.step())
                wait_alone(v, steps_sem, n.total())
                for t in range(TT):
                    v.bn_aggr(out=moments[:, t, :], in_=stats[:, t, :]).then_inc(steps_sem, n.step())
                v.wait_ge(steps_sem, n.total())
                v.tensor_scalar(ln_v[:, :], moments[:, :, 1], LN_EPS, None, ALU.add).then_inc(steps_sem, n.step())
                v.wait_ge(steps_sem, n.total())
                v.tensor_scalar(ln_a[:, :].bitcast(I32), ln_v[:, :].bitcast(I32), 1, None,
                                ALU.logical_shift_right).then_inc(steps_sem, n.step())
                v.wait_ge(steps_sem, n.total())
                v.tensor_scalar(ln_y[:, :].bitcast(I32), ln_a[:, :].bitcast(I32), -1.0, float(RSQRT_SEED),
                                ALU.mult, ALU.add).then_inc(steps_sem, n.step())
                for _ in range(NEWTON):
                    v.wait_ge(steps_sem, n.total())
                    v.tensor_tensor(ln_a[:, :], ln_y[:, :], ln_v[:, :], ALU.mult).then_inc(steps_sem, n.step())
                    v.wait_ge(steps_sem, n.total())
                    v.tensor_tensor(ln_a[:, :], ln_a[:, :], ln_y[:, :], ALU.mult).then_inc(steps_sem, n.step())
                    v.wait_ge(steps_sem, n.total())
                    v.tensor_scalar(ln_a[:, :], ln_a[:, :], -0.5, 1.5, ALU.mult, ALU.add).then_inc(steps_sem, n.step())
                    v.wait_ge(steps_sem, n.total())
                    v.tensor_tensor(ln_y[:, :], ln_y[:, :], ln_a[:, :], ALU.mult).then_inc(steps_sem, n.step())
                v.wait_ge(steps_sem, n.total())
                for t in range(TT):
                    v.tensor_scalar(h[:, t, :], xin[:, t, :], moments[:, t, 0:1], ln_y[:, t:t + 1],
                                    ALU.subtract, ALU.mult).then_inc(steps_sem, n.step())
                assert n.steps == LN_STEPS

            def split(batch, section, i, nth, which, half):
                n = Count(4 * tile_count(batch, section, i, nth))
                full = weight[:, nth, :]
                v.wait_ge(split_steps, n.total())
                v.wait_ge(weighted, tile_count(batch, section, i, nth) + 1)
                v.wait_ge(parts_stored[nth], STORES * (2 * NC * batch + TILES_BEFORE[section] // 2 + i))
                parts_of = parts[nth]
                if which:
                    scale = amp[:, half:half + 1]
                    v.tensor_scalar(parts_of[:, 0, :], full, scale, None, ALU.mult).then_inc(split_steps, n.step())
                    v.wait_ge(split_steps, n.total())
                    v.scalar_tensor_tensor(out=rest[:, :], in0=full, scalar=scale, in1=parts_of[:, 0, :],
                                           op0=ALU.mult, op1=ALU.subtract).then_inc(split_steps, n.step())
                else:
                    v.tensor_copy(parts_of[:, 0, :], full).then_inc(split_steps, n.step())
                    v.wait_ge(split_steps, n.total())
                    v.tensor_tensor(rest[:, :], full, parts_of[:, 0, :], ALU.subtract).then_inc(split_steps, n.step())
                v.wait_ge(split_steps, n.total())
                v.tensor_copy(parts_of[:, 1, :], rest[:, :]).then_inc(split_steps, n.step())
                v.wait_ge(split_steps, n.total())
                v.tensor_tensor(parts_of[:, 2, :], rest[:, :], parts_of[:, 1, :], ALU.subtract).then_inc(split_steps, n.step())
                assert n.steps == 4

            def prep_chunk(batch, section, i, between=None):
                steps = SECTIONS[section][0]
                if steps[0][0] == "turn":
                    v.wait_ge(prep_x_loaded, 16 * (NC * batch + i + 1))
                    layernorm(NC * batch + i, x_prep, prep_ln)
                for k, (kind, *which) in enumerate(steps):
                    nth = k - steps.index(next(x for x in steps if x[0] == kind))
                    if section == "first":
                        bank = ps_scores[:, k // BANKS_PER_GROUP, k % BANKS_PER_GROUP, :]
                    else:
                        bank = ps_step[:, :]
                    if kind == "project" and nth == 0:
                        v.wait_ge(squared, tile_count(batch, section, i))
                    if kind == "value" and nth == 0 and between:
                        between()
                    if kind == "distance" and nth == 0:
                        v.wait_ge(split_steps, 4 * tile_count(batch, section, i))
                    if kind == "value" and nth == 0:
                        v.wait_ge(vals_staged, NC * STAGES * batch)
                    v.wait_ge(prep_mm, prep_count(batch, section, i, k) + 1)
                    if kind == "turn":
                        v.tensor_copy(h_t[:, nth, bass.ds(i * CHUNK, CHUNK)], bank).then_inc(prep_free, 1)
                    elif kind == "project":
                        v.tensor_copy(qk[:, nth, :], bank).then_inc(prep_free, 1)
                    elif kind == "value":
                        v.tensor_copy(v_all[:, bass.ds(i * TT + 2 * nth, 2), :],
                                      bank.rearrange("p (n d) -> p n d", d=D)).then_inc(prep_free, 1)
                    else:
                        v.tensor_scalar(weight[:, nth, :], bank, cen_sq[:, which[1]:which[1] + 1], 0.0,
                                        ALU.add, ALU.max).then_inc(prep_free, 1)
                for nth, (_, which, half) in enumerate(x for x in steps if x[0] == "distance"):
                    split(batch, section, i, nth, which, half)

            def ffn_chunk(batch, i, steps=WHOLE):
                nth = NC * batch + i

                def done(k):
                    v.wait_ge(ffn_mm, ffn_count(batch, i, k) + 1)

                if 0 in steps:
                    v.wait_ge(ffn_x_loaded, 16 * (nth + 1))
                    for pair in range(2):
                        rows = x_ffn[:, 2 * pair:2 * pair + 2, :]
                        done(pair)
                        v.tensor_tensor(rows, ffn_bank(batch, i, pair).rearrange("p (n d) -> p n d", d=D), rows,
                                        ALU.add).then_inc(ffn_free, 1)
                    v.wait_ge(ffn_free, ffn_count(batch, i, 2))
                    v.wait_ge(out_stored, 16 * nth)
                    layernorm(nth, x_ffn, ffn_ln)
                    n = Count(9 * nth)
                    v.wait_ge(mix_steps, n.total())
                    v.tensor_copy(h2_t[:, :, 0:1], h2_t[:, :, CHUNK:CHUNK + 1]).then_inc(mix_steps, n.step())
                    v.wait_ge(mix_steps, n.total())
                    for half in range(HALVES):
                        done(2 + half)
                        v.tensor_copy(h2_t[:, half, 1:1 + CHUNK], ffn_bank(batch, i, 2 + half)).then_inc(ffn_free, 1)
                    v.wait_ge(ffn_free, ffn_count(batch, i, 4))
                    for which, dst in ((0, mixed_r), (1, mixed_k)):
                        for half in range(HALVES):
                            v.wait_ge(mix_steps, n.total())
                            v.tensor_scalar(tmp[:, :], h2_t[:, half, 0:CHUNK], one_minus_mu[:, which, half:half + 1], None,
                                            ALU.mult).then_inc(mix_steps, n.step())
                            v.wait_ge(mix_steps, n.total())
                            v.scalar_tensor_tensor(out=dst[:, half, :], in0=h2_t[:, half, 1:1 + CHUNK],
                                                   scalar=mu[:, which, half:half + 1], in1=tmp[:, :],
                                                   op0=ALU.mult, op1=ALU.add).then_inc(mix_steps, n.step())
                    assert n.steps == 9
                if FFN_STEPS - 1 in steps:
                    for pair in range(2):
                        done(4 + pair)
                        v.tensor_scalar(gate_in[:, 2 * pair:2 * pair + 2, :],
                                        ffn_bank(batch, i, 4 + pair).rearrange("p (n d) -> p n d", d=D), -87.0, None,
                                        ALU.max).then_inc(ffn_free, 1)
                    for half in range(HALVES):
                        done(6 + half)
                        v.tensor_scalar(k_act[:, half, :], ffn_bank(batch, i, 6 + half), 0.0, None, ALU.max).then_inc(ffn_free, 1)
                    n = Count(4 * nth)
                    v.wait_ge(gate_exp, 2 * (nth + 1))
                    v.tensor_scalar(gate[:, :, :], gate[:, :, :], 1.0, None, ALU.add).then_inc(gate_steps, n.step())
                    v.wait_ge(gate_steps, n.total())
                    for pair in range(2):
                        rows = gate[:, 2 * pair:2 * pair + 2, :]
                        v.reciprocal(rows, rows).then_inc(gate_steps, n.step())
                    v.wait_ge(gate_steps, n.total())
                    for pair in range(2):
                        done(8 + pair)
                        v.tensor_tensor(gate_in[:, 2 * pair:2 * pair + 2, :],
                                        ffn_bank(batch, i, 8 + pair).rearrange("p (n d) -> p n d", d=D), gate[:, 2 * pair:2 * pair + 2, :],
                                        ALU.mult).then_inc(ffn_free, 1)
                    v.wait_ge(ffn_free, ffn_count(batch, i, FFN_STEPS))
                    v.tensor_tensor(gate_in[:, :, :], gate_in[:, :, :], x_ffn[:, :, :], ALU.add).then_inc(gate_steps, n.step())
                    assert n.steps == 4

            def clear_carry(batch, prepared):
                for stored in parts_stored:
                    wait_alone(v, stored, STORES * 2 * NC * prepared)
                v.memset(h2_t[:, :, CHUNK:CHUNK + 1], 0.0).then_inc(carry_cleared, 1)
                wait_alone(v, carry_cleared, batch + 1)

            def normalise(b, s, i):
                half, odd = s // 2, s % 2
                u = UNITS * b + NC * s + i
                n = Count(norm_count(b, s, i))
                dst = heads_of(b)[:, half, bass.ds(i * CHUNK, CHUNK)]
                v.wait_ge(chunk_normed, u)
                v.wait_ge(pv_done, u + 1)
                v.tensor_copy(o_raw[:, :], ps_pv[:, :]).then_inc(pv_free, 1)
                wait_alone(v, pv_free, u + 1)
                v.stream_shuffle(den[:, :], o_raw[:, :], odd_den if odd else even_den).then_inc(norm_steps, n.step())
                v.wait_ge(norm_steps, n.total())
                v.reciprocal(den[:, :], den[:, :]).then_inc(norm_steps, n.step())
                v.wait_ge(norm_steps, n.total())
                if not odd:
                    v.tensor_tensor(dst, o_raw[:, :], den[:, :], ALU.mult).then_inc(chunk_normed, 1)
                else:
                    v.tensor_tensor(o_raw[:, :], o_raw[:, :], den[:, :], ALU.mult).then_inc(norm_steps, n.step())
                    v.wait_ge(norm_steps, n.total())
                    v.tensor_scalar(o_raw[:, :], o_raw[:, :], rowmask[:, 1:2], None, ALU.mult).then_inc(norm_steps, n.step())
                    v.wait_ge(norm_steps, n.total())
                    v.scalar_tensor_tensor(out=dst, in0=dst, scalar=rowmask[:, 0:1], in1=o_raw[:, :],
                                           op0=ALU.mult, op1=ALU.add).then_inc(chunk_normed, 1)

            def shift_pass(stage_no):
                with v.Fori(0, KT) as qt:
                    for c in range(HEADS_AT_ONCE):
                        v.wait_ge(max_free, MAX_STEPS * stage_no + HEADS_AT_ONCE * (NC + 1) * qt + (NC + 1) * c)
                        for kc in range(NC):
                            v.wait_ge(max_mm, MAX_TILES * stage_no + HEADS_AT_ONCE * NC * qt + NC * c + kc + 1)
                            v.tensor_reduce(tile_max[:, kc:kc + 1], ps_step[:, :], AX.X, ALU.max).then_inc(max_free, 1)
                        v.wait_ge(max_free, MAX_STEPS * stage_no + HEADS_AT_ONCE * (NC + 1) * qt + (NC + 1) * c + NC)
                        v.tensor_reduce(row_max[:, bass.ds(c * KT + qt, 1)], tile_max[:, :], AX.X, ALU.max,
                                        negate=True).then_inc(max_free, 1)
                v.wait_ge(max_mm, MAX_TILES * (stage_no + 1))
                v.tensor_copy(max_rows[:, :], ps_step[0:HEADS_AT_ONCE * KT, 0:P]).then_inc(max_free, 1)

            v.memset(vals[:, :, :, :, :], 1.0).then_inc(ones_set, 1)
            n = Count(0)

            def after():
                v.wait_ge(setup_dve, n.total())

            v.wait_ge(prep_x_loaded, 16)
            layernorm(0, x_prep, prep_ln)
            v.wait_ge(consts_loaded, 16 * N_CONSTS)
            v.wait_ge(setup_act, 3)
            v.tensor_scalar(params[:, 1:2], params[:, 1:2], 0.1, 10.0, ALU.max, ALU.min).then_inc(setup_dve, n.step())
            after()
            v.reciprocal(params[:, 1:2], params[:, 1:2]).then_inc(setup_dve, n.step())
            v.tensor_scalar(amp[:, :], amp[:, :], 1e-6, 10.0, ALU.max, ALU.min).then_inc(setup_dve, n.step())
            after()
            v.tensor_scalar(amp[:, :], amp[:, :], params[:, 1:2], None, ALU.mult).then_inc(setup_dve, n.step())
            after()
            assert n.steps == SETUP_AMP
            v.wait_ge(setup_pe, 1)
            v.tensor_copy(bound[:, :], ps_setup[:, 0:HALVES]).then_inc(setup_dve, n.step())
            after()
            assert n.steps == SETUP_BOUND
            for half in range(HALVES):
                v.tensor_scalar(shift[:, half, :], bound[:, half:half + 1].broadcast_to([P, CHUNK]), -1.0, None,
                                ALU.mult).then_inc(setup_dve, n.step())
            assert n.steps == SETUP_SHIFT
            v.tensor_scalar(params[:, 0:1], params[:, 0:1], 1.0, None, ALU.add).then_inc(setup_dve, n.step())
            after()
            v.reciprocal(params[:, 0:1], params[:, 0:1]).then_inc(setup_dve, n.step())
            after()
            v.tensor_scalar(params[:, 0:1], params[:, 0:1], 0.2, None, ALU.mult).then_inc(setup_dve, n.step())
            after()
            for cen, dlt in ((cen_t, del_t), (cen_n, del_n)):
                v.scalar_tensor_tensor(out=cen[:, :, :], in0=dlt[:, :, :], scalar=params[:, 0:1], in1=cen[:, :, :],
                                       op0=ALU.mult, op1=ALU.add).then_inc(setup_dve, n.step())
            after()
            v.tensor_tensor(del_n[:, :, :], cen_n[:, :, :], cen_n[:, :, :], ALU.mult).then_inc(setup_dve, n.step())
            v.tensor_scalar(cen_t[:, :, :], cen_t[:, :, :], -2.0, None, ALU.mult).then_inc(setup_dve, n.step())
            after()
            v.tensor_reduce(cen_sq[:, :], del_n[:, :, :], AX.X, ALU.add).then_inc(setup_dve, n.step())
            for half in range(HALVES):
                v.tensor_tensor(cross[:, half, :].rearrange("p (h s) -> p h s", s=S),
                                headmask[:, :].rearrange("p (h s) -> p h s", s=S),
                                cen_t[:, half:half + 1, :].broadcast_to([P, P // S, S]),
                                ALU.mult).then_inc(setup_dve, n.step())
            v.tensor_scalar(inv_var[:, :], inv_var[:, :], 0.01, 2.0, ALU.max, ALU.min).then_inc(setup_dve, n.step())
            after()
            v.tensor_tensor(inv_var[:, :], inv_var[:, :], inv_var[:, :], ALU.mult).then_inc(setup_dve, n.step())
            after()
            v.tensor_scalar(inv_var[:, :], inv_var[:, :], 1e-8, None, ALU.add).then_inc(setup_dve, n.step())
            after()
            v.reciprocal(inv_var[:, :], inv_var[:, :]).then_inc(setup_dve, n.step())
            after()
            v.tensor_scalar(inv_var[:, :], inv_var[:, :], -0.5, None, ALU.mult).then_inc(setup_dve, n.step())
            v.tensor_scalar(one_minus_mu[:, :, :], mu[:, :, :], -1.0, 1.0, ALU.mult, ALU.add).then_inc(setup_dve, n.step())
            v.wait_ge(setup_pe, 2)
            v.tensor_reduce(flag_f[:, 0:1], ps_setup[0:1, 0:HALVES * P], AX.X, ALU.max).then_inc(setup_dve, n.step())
            after()
            v.tensor_scalar(flag[:, :], flag_f[:, 0:1], SAFE_BOUND, None, ALU.is_gt).then_inc(setup_dve, n.step())
            after()
            assert n.steps == SETUP_STEPS, n.steps
            unsafe = v.value_load(flag[0:1, 0:1], min_val=0, max_val=1)

            def next_layernorm(i):
                v.wait_ge(prep_x_loaded, 16 * (i + 2))
                v.wait_ge(first_turned, HALVES * (i + 1))
                layernorm(i + 1, x_prep, prep_ln)

            with v.Fori(0, NC - 1) as i:
                prep_chunk(0, "first", i, between=lambda: next_layernorm(i))
            prep_chunk(0, "first", NC - 1)
            with v.If(unsafe == 1):
                shift_pass(0)

            def unit(b, s, i, prep, finish=None, shifts=True):
                if shifts:
                    with v.If(unsafe * i == NC - 1):
                        shift_pass(STAGES * b + s + 1)
                if finish or prep:
                    v.wait_ge(chunk_normed, UNITS * b + NC * s + i)
                if finish:
                    ffn_chunk(*finish)
                if prep:
                    prep_chunk(*prep, i)
                    if prep[1] != 3:
                        v.wait_ge(split_steps, 4 * tile_count(*prep, i + 1))
                normalise(b, s, i)

            def body(b, prep, ffn):
                for s in range(STAGES):
                    if s == 0 and ffn:
                        clear_carry(b - 1, b + 1)
                    if s == 1 and ffn and prep:
                        wait_alone(v, out_stored, 16 * NC * b)
                    if s == STAGES - 1 and not prep:
                        clear_carry(b, NB)
                        unit(b, s, 0, None, shifts=False)
                        with v.Fori(1, NC) as i:
                            unit(b, s, i, None, finish=(b, i - 1, WHOLE), shifts=False)
                    elif s < 2 and not prep:
                        with v.Fori(0, NC // 2) as pair:
                            for n, steps in enumerate((UPPER, LOWER)):
                                unit(b, s, 2 * pair + n, None, finish=(b - 1, NC // 2 * s + pair, steps))
                    else:
                        with v.Fori(0, NC) as i:
                            unit(b, s, i, prep_beside(b, s, prep, ffn), finish=(b - 1, i, WHOLE) if s == 0 and ffn else None)

            batches(v, body)
            v.wait_ge(chunk_normed, UNITS * NB)
            ffn_chunk(NB - 1, NC - 1)


N_CONSTS = 18
SETUP_AMP = 4
SETUP_BOUND = 5
SETUP_SHIFT = 7
SETUP_STEPS = 25


def kernel(L0_attn_x, L0_attn_splat_centers, L0_attn_splat_deltas, L0_attn_splat_log_scales,
           L0_attn_splat_log_amplitudes, L0_attn_movement_scale, L0_attn_temperature, L0_attn_qkv_w,
           L0_attn_out_w, L0_ffn_W_r, L0_ffn_W_k, L0_ffn_W_v, L0_ffn_mu_r, L0_ffn_mu_k):
    import numpy as np
    import concourse.bacc as bacc
    from concourse.bass_utils import run_bass_kernel_spmd

    def laid(a, shape=None):
        a = np.asarray(a)
        return np.ascontiguousarray(a if shape is None else a.reshape(shape))

    heads, splats, hd = np.shape(L0_attn_splat_centers)
    x = laid(L0_attn_x)
    d = x.shape[2]

    def dims_first(a):
        return laid(np.transpose(np.asarray(a), (0, 2, 1)), (heads * hd, splats))

    def columns(a):
        return laid(laid(a, (-1, P)).T)

    row = np.arange(P)
    arrays = {
        "x": x,
        "qkv_wT": laid(np.asarray(L0_attn_qkv_w).T),
        "out_wT": laid(np.asarray(L0_attn_out_w).T),
        "r_wT": laid(np.asarray(L0_ffn_W_r).T),
        "k_wT": laid(np.asarray(L0_ffn_W_k).T),
        "v_wT": laid(np.asarray(L0_ffn_W_v).T),
        "cen_hds": dims_first(L0_attn_splat_centers),
        "del_hds": dims_first(L0_attn_splat_deltas),
        "cen_hsd": laid(L0_attn_splat_centers, (heads * splats, hd)),
        "del_hsd": laid(L0_attn_splat_deltas, (heads * splats, hd)),
        "log_scales": columns(L0_attn_splat_log_scales),
        "log_amps": columns(L0_attn_splat_log_amplitudes),
        "movement": laid(L0_attn_movement_scale, (1, 1)),
        "temperature": laid(L0_attn_temperature, (1, 1)),
        "mu_r": columns(L0_ffn_mu_r),
        "mu_k": columns(L0_ffn_mu_k),
        "ident_in": np.eye(P, dtype=np.float32),
        "headmask_in": (row[:, None] // hd == row[None, :] // hd).astype(np.float32),
        "rowmask_in": np.stack([row // hd % 2 == 0, row // hd % 2 == 1], axis=1).astype(np.float32),
    }
    nc = bacc.Bacc("TRN2", target_bir_lowering=False, num_devices=1)
    args = [nc.dram_tensor(name, a.shape, mybir.dt.from_np(a.dtype), kind="ExternalInput").ap()
            for name, a in arrays.items()]
    out = nc.dram_tensor("out", x.shape, F32, kind="ExternalOutput").ap()
    preln_block(nc, *args, out)
    result = run_bass_kernel_spmd(nc, [arrays], core_ids=[0])
    return result.results[0]["out"]
```
